# Optimizing a Trainium2 kernel written in Bass

```python
import numpy as np
import jax
import jax.numpy as jnp

def _softmax(x, axis=-1):
    return jax.nn.softmax(x, axis=axis)
def _gelu(x):
    return jax.nn.gelu(x, approximate=True)
def _silu(x):
    return jax.nn.silu(x)
def _sigmoid(x):
    return jax.nn.sigmoid(x)
def _layernorm(x, axis=-1, eps=1e-5):
    m = jnp.mean(x, axis=axis, keepdims=True)
    v = jnp.var(x, axis=axis, keepdims=True)
    return (x - m) / jnp.sqrt(v + eps)
def _scatter_add(tgt, idx, src, axis=0):
    return tgt.at[idx].add(src)
def _segment_sum(src, seg, n):
    return jax.ops.segment_sum(src, seg, n)

kernel_name = 'mk_conv_attn_hybrid_d2_conv_nchw128_c48a10'

def setup_inputs(seed: int = 0):
    np.random.seed(seed)
    _w = jnp.asarray
    def _rec_inputs():
        import jax
        import jax.numpy as jnp
        _gk = jax.random.key(seed)
        x = -0.0005207 + 1.001 * jax.random.normal(jax.random.fold_in(_gk, 1), (4, 128, 64, 64), jnp.float32)
        return x
    x = _rec_inputs()
    def _L0_conv_setup():
        import jax, jax.numpy as jnp
        import numpy as np
        EPS = 1e-05
        GROUPS = 32

        def group_norm(x, w, b):
            B, C, H, W = x.shape
            g = x.reshape(B, GROUPS, C // GROUPS, H, W)
            mean = g.mean(axis=(2, 3, 4), keepdims=True)
            var = g.var(axis=(2, 3, 4), keepdims=True)
            g = (g - mean) * jax.lax.rsqrt(var + EPS)
            g = g.reshape(B, C, H, W)
            return g * w[None, :, None, None] + b[None, :, None, None]
        key = jax.random.key(seed)
        ks = jax.random.split(key, 8)
        B, C, H, W = (4, 128, 64, 64)
        s = 1.0 / np.sqrt(C)
        return {'x': jax.random.normal(ks[0], (B, C, H, W), jnp.float32), 'norm_w': jax.random.normal(ks[1], (C,), jnp.float32), 'norm_b': jax.random.normal(ks[2], (C,), jnp.float32), 'Wq': jax.random.normal(ks[3], (C, C), jnp.float32) * s, 'bq': jnp.zeros((C,), jnp.float32), 'Wk': jax.random.normal(ks[4], (C, C), jnp.float32) * s, 'bk': jnp.zeros((C,), jnp.float32), 'Wv': jax.random.normal(ks[5], (C, C), jnp.float32) * s, 'bv': jnp.zeros((C,), jnp.float32), 'Wo': jax.random.normal(ks[6], (C, C), jnp.float32) * s, 'bo': jnp.zeros((C,), jnp.float32)}
    _L0_conv_all = _L0_conv_setup()
    _L0_conv_in = {k: v for k, v in _L0_conv_all.items() if k in ('norm_w', 'norm_b', 'Wq', 'bq', 'Wk', 'bk', 'Wv', 'bv', 'Wo', 'bo', )}
    del _L0_conv_all

    def _L1_attn_setup():
        import jax, jax.numpy as jnp
        import numpy as np
        HEADS = 8
        DIM = 128
        key = jax.random.key(seed)
        k1, k2, k3 = jax.random.split(key, 3)
        b, t, d, h = (4, 4096, DIM, HEADS)
        x = jax.random.normal(k1, (b, t, d), dtype=jnp.float32)
        W_kv = jax.random.normal(k2, (h * d * 2, d), dtype=jnp.float32) * (1.0 / np.sqrt(d))
        q_proj = jax.random.normal(k3, (h, d), dtype=jnp.float32) * (1.0 / np.sqrt(d))
        return {'x': x, 'W_kv': W_kv, 'q_proj': q_proj}
    _L1_attn_all = _L1_attn_setup()
    _L1_attn_in = {k: v for k, v in _L1_attn_all.items() if k in ('W_kv', 'q_proj', )}
    del _L1_attn_all

    def _L1_ffn_setup():
        import jax, jax.numpy as jnp
        import numpy as np
        B, N, D, C, E, K = (8, 8192, 128, 128, 8, 2)
        key = jax.random.key(seed)
        k0, k1, k2 = jax.random.split(key, 3)
        x = jax.random.normal(k0, (B, N, D), dtype=jnp.float32)
        router_w = jax.random.normal(k1, (D, E), dtype=jnp.float32) * 0.05
        router_b = jnp.zeros((E,), dtype=jnp.float32)
        expert_w = jax.random.normal(k2, (E, D, C), dtype=jnp.float32) * (1.0 / np.sqrt(D))
        expert_b = jnp.zeros((E, C), dtype=jnp.float32)
        return {'x': x, 'router_w': router_w, 'router_b': router_b, 'expert_w': expert_w, 'expert_b': expert_b}
    _L1_ffn_all = _L1_ffn_setup()
    _L1_ffn_in = {k: v for k, v in _L1_ffn_all.items() if k in ('router_w', 'router_b', 'expert_w', 'expert_b', )}
    del _L1_ffn_all

    return {
        "x": x,
        "L0_conv_norm_w": _L0_conv_in["norm_w"],
        "L0_conv_norm_b": _L0_conv_in["norm_b"],
        "L0_conv_Wq": _L0_conv_in["Wq"],
        "L0_conv_bq": _L0_conv_in["bq"],
        "L0_conv_Wk": _L0_conv_in["Wk"],
        "L0_conv_bk": _L0_conv_in["bk"],
        "L0_conv_Wv": _L0_conv_in["Wv"],
        "L0_conv_bv": _L0_conv_in["bv"],
        "L0_conv_Wo": _L0_conv_in["Wo"],
        "L0_conv_bo": _L0_conv_in["bo"],
        "L1_attn_W_kv": _L1_attn_in["W_kv"],
        "L1_attn_q_proj": _L1_attn_in["q_proj"],
        "L1_ffn_router_w": _L1_ffn_in["router_w"],
        "L1_ffn_router_b": _L1_ffn_in["router_b"],
        "L1_ffn_expert_w": _L1_ffn_in["expert_w"],
        "L1_ffn_expert_b": _L1_ffn_in["expert_b"],
    }

def reference(x, L0_conv_norm_w, L0_conv_norm_b, L0_conv_Wq, L0_conv_bq, L0_conv_Wk, L0_conv_bk, L0_conv_Wv, L0_conv_bv, L0_conv_Wo, L0_conv_bo, L1_attn_W_kv, L1_attn_q_proj, L1_ffn_router_w, L1_ffn_router_b, L1_ffn_expert_w, L1_ffn_expert_b):
    import jax
    import jax.numpy as jnp
    def _L0_conv_ref(x, norm_w, norm_b, Wq, bq, Wk, bk, Wv, bv, Wo, bo):
        import jax, jax.numpy as jnp
        import numpy as np
        EPS = 1e-05
        GROUPS = 32

        def group_norm(x, w, b):
            B, C, H, W = x.shape
            g = x.reshape(B, GROUPS, C // GROUPS, H, W)
            mean = g.mean(axis=(2, 3, 4), keepdims=True)
            var = g.var(axis=(2, 3, 4), keepdims=True)
            g = (g - mean) * jax.lax.rsqrt(var + EPS)
            g = g.reshape(B, C, H, W)
            return g * w[None, :, None, None] + b[None, :, None, None]
        B, C, H, W = x.shape
        h = group_norm(x, norm_w, norm_b)
        h = h.transpose(0, 2, 3, 1)
        q = jnp.einsum('bhwc,cd->bhwd', h, Wq) + bq
        k = jnp.einsum('bhwc,cd->bhwd', h, Wk) + bk
        v = jnp.einsum('bhwc,cd->bhwd', h, Wv) + bv
        N = H * W
        qf = q.reshape(B, N, C)
        kf = k.reshape(B, N, C)
        vf = v.reshape(B, N, C)
        scores = jnp.einsum('bnc,bmc->bnm', qf, kf) * C ** (-0.5)
        attn = jax.nn.softmax(scores, axis=-1)
        o = jnp.einsum('bnm,bmc->bnc', attn, vf)
        o = jnp.einsum('bnc,cd->bnd', o, Wo) + bo
        o = o.reshape(B, H, W, C).transpose(0, 3, 1, 2)
        return x + o

    def _L1_attn_ref(x, W_kv, q_proj):
        import jax, jax.numpy as jnp
        import numpy as np
        HEADS = 8
        DIM = 128
        b, t, d = x.shape
        h = q_proj.shape[0]
        kv = jnp.einsum('btd,ed->bte', x, W_kv).reshape(b, t, h, d, 2)
        kv = jax.nn.silu(kv)
        k, v = (kv[..., 0], kv[..., 1])
        s = jnp.einsum('hd,bthd->bth', q_proj, k)
        m_A = jax.lax.cummax(s, axis=1)
        exp_scores = jnp.exp(s - m_A)
        u_A = jnp.cumsum(exp_scores, axis=1)
        w_A = jnp.cumsum(exp_scores[..., None] * v, axis=1)
        output = w_A / u_A[..., None]
        return output.mean(axis=2)

    def _L1_ffn_ref(x, router_w, router_b, expert_w, expert_b):
        import jax, jax.numpy as jnp
        import numpy as np
        B, N, D, C, E, K = (8, 8192, 128, 128, 8, 2)
        router_probs = jax.nn.softmax(x @ router_w + router_b, axis=-1)
        top_p, top_i = jax.lax.top_k(router_probs, K)
        top_p = top_p / jnp.sum(top_p, axis=-1, keepdims=True)
        expert_out = jnp.einsum('bnd,edc->bnec', x, expert_w) + expert_b
        gathered = jnp.take_along_axis(expert_out, top_i[..., None], axis=2)
        return jnp.einsum('bnk,bnkc->bnc', top_p, gathered)

    def _gn(v, G=32, eps=1e-5):
        B_, C_, H_, W_ = v.shape
        g = v.reshape(B_, G, C_ // G, H_, W_)
        m = jnp.mean(g, axis=(2, 3, 4), keepdims=True)
        s = jnp.var(g, axis=(2, 3, 4), keepdims=True)
        return ((g - m) / jnp.sqrt(s + eps)).reshape(v.shape)

    def _ln_c(v, eps=1e-6):
        m = jnp.mean(v, axis=1, keepdims=True)
        s = jnp.var(v, axis=1, keepdims=True)
        return (v - m) / jnp.sqrt(s + eps)

    def _ln_t(v, eps=1e-5):
        m = jnp.mean(v, axis=-1, keepdims=True)
        s = jnp.var(v, axis=-1, keepdims=True)
        return (v - m) / jnp.sqrt(s + eps)

    def _to_tokens(v):
        B_, C_, H_, W_ = v.shape
        return v.reshape(B_, C_, H_ * W_).transpose(0, 2, 1)
    def _from_tokens(t, like):
        B_, C_, H_, W_ = like.shape
        return t.transpose(0, 2, 1).reshape(B_, C_, H_, W_)

    x = _L0_conv_ref(x, L0_conv_norm_w, L0_conv_norm_b, L0_conv_Wq, L0_conv_bq, L0_conv_Wk, L0_conv_bk, L0_conv_Wv, L0_conv_bv, L0_conv_Wo, L0_conv_bo)
    t = _to_tokens(x)
    t = t + _L1_attn_ref(_ln_t(t), L1_attn_W_kv, L1_attn_q_proj)
    t = t + _L1_ffn_ref(_ln_t(t), L1_ffn_router_w, L1_ffn_router_b, L1_ffn_expert_w, L1_ffn_expert_b)
    x = _from_tokens(t, x)
    return x


_drawn_inputs = setup_inputs


def setup_inputs(seed=0):
    import zlib

    import numpy as np

    out = dict(_drawn_inputs(seed))
    spreads = {'L0_conv_bq': (0.0, 0.1),
     'L0_conv_bk': (0.0, 0.8),
     'L0_conv_bv': (0.0, 0.1),
     'L0_conv_bo': (0.0, 0.1),
     'L1_ffn_router_b': (0.0, 0.1),
     'L1_ffn_expert_b': (0.0, 0.1)}
    factors = {'L1_attn_q_proj': 2.844}
    for name, (base, spread) in spreads.items():
        noise = np.random.default_rng([zlib.crc32(name.encode()), seed]).standard_normal(out[name].shape)
        drawn = base * np.exp(spread * noise) if base else spread * noise
        out[name] = jnp.asarray(drawn.astype(out[name].dtype))
    for name, factor in factors.items():
        out[name] = (out[name] * factor).astype(out[name].dtype)
    return out
```

```python
from contextlib import ExitStack

import concourse.bass as bass
from concourse import mybir

F32 = mybir.dt.float32
F32R = mybir.dt.float32r
ALU = mybir.AluOpType
ACT = mybir.ActivationFunctionType
AX = mybir.AxisListType
ds = bass.ds

C = 128
BANK = 512
QB = 256
QT = QB // C
GROUPS = 32
EPS = 1e-5


def softmax_attention(nc, x, norm_w, norm_b, Wq, bq, Wk, bk, Wv, bv, Wo, bo, t_dram):
    B, _, H, W = x.shape
    N = H * W
    NB = N // QB
    KT = N // C
    STEPS = KT // 2
    KCH = N // BANK
    GRP = QT * KCH // 2
    XCH = 4
    XW = N // XCH
    SCALE = float(C) ** -0.5
    AHEAD = 3
    x_v = x.rearrange("b c h w -> b c (h w)")

    with ExitStack() as ctx:
        def sb(name, shape, dt=F32):
            return ctx.enter_context(nc.sbuf_tensor(name, shape, dt))

        def sem(name):
            return ctx.enter_context(nc.semaphore(name))

        xb = sb("xb", [C, 2, N])
        hn = sb("hn", [C, N])
        k_hi, k_lo = sb("k_hi", [C, N], F32R), sb("k_lo", [C, N], F32R)
        v_hi, v_lo = sb("v_hi", [C, KT, C], F32R), sb("v_lo", [C, KT, C], F32R)
        s_sb = sb("s_sb", [C, 2, QT, N])
        q_hi, q_lo = sb("q_hi", [C, 2, QB], F32R), sb("q_lo", [C, 2, QB], F32R)
        pt_hi, pt_lo = sb("pt_hi", [C, 2, 2, QB], F32R), sb("pt_lo", [C, 2, 2, QB], F32R)
        wq, wk, wv, wo = (sb(n, [C, C]) for n in ("wq", "wk", "wv", "wo"))
        wvo, wvT = sb("wvo", [C, C]), sb("wvT", [C, C])
        ident, gavg = sb("ident", [C, C]), sb("gavg", [C, C])
        cols = sb("cols", [C, 6])
        gnw, gnb, bqc, bkc, bvc, boc = (cols[:, i:i + 1] for i in range(6))
        bvo = sb("bvo", [C, 1])
        bn = sb("bn", [C, KCH, 6])
        mom = sb("mom", [C, 2])
        gst = sb("gst", [C, 8])
        ga, gb = sb("ga", [C, 1]), sb("gb", [C, 1])
        gtmp = sb("gtmp", [C, 1])
        epsc = sb("epsc", [C, 1])
        mx = sb("mx", [C, 2, QT, GRP // QT])
        nmax = sb("nmax", [C, 2, QT])
        rsum = sb("rsum", [C, 2, QT, XCH])
        rden = sb("rden", [C, 2, QT])
        rinv = sb("rinv", [C, 2, QT])
        rb_sb = sb("rb_sb", [C, QB])
        on = sb("on", [C, QB])

        s_ps = ctx.enter_context(nc.psum_tensor("s_ps", [C, 2, 2, BANK], F32))
        pt_ps = ctx.enter_context(nc.psum_tensor("pt_ps", [C, 2, 2, QB], F32))
        o_ps = ctx.enter_context(nc.psum_tensor("o_ps", [C, BANK], F32))
        m_ps = ctx.enter_context(nc.psum_tensor("m_ps", [C, BANK], F32))

        w_in, x_in, t_out = sem("w_in"), sem("x_in"), sem("t_out")
        const_a, const_b = sem("const_a"), sem("const_b")
        wt_pe, wt_cp, wp_pe, wp_cp = sem("wt_pe"), sem("wt_cp"), sem("wp_pe"), sem("wp_cp")
        bn_done, gn_step, gn_pe, gn_ln, gn_rs = sem("bn_done"), sem("gn_step"), sem("gn_pe"), sem("gn_ln"), sem("gn_rs")
        h_done = sem("h_done")
        kv_pe, kv_hi, kv_lo = sem("kv_pe"), sem("kv_hi"), sem("kv_lo")
        q_pe, q_h, q_l = sem("q_pe"), sem("q_h"), sem("q_l")
        sc_pe, sc_cp, mx_done = sem("sc_pe"), sem("sc_cp"), sem("mx_done")
        exp_done = sem("exp_done")
        tr_pe, p_hi, p_lo, pv_pe = sem("tr_pe"), sem("p_hi"), sem("p_lo"), sem("pv_pe")
        den_done, inv_done, rb_pe, rb_cp = sem("den_done"), sem("inv_done"), sem("rb_pe"), sem("rb_cp")
        on_done, t_done = sem("on_done"), sem("t_done")

        KV = KCH + KT // 4
        block = ctx.enter_context(nc.Block())

        def walk(eng, image, blk, drain=None):
            with eng.Fori(0, B) as b:
                image(b)
                for p in range(2):
                    blk(b, b * NB + p, p, p, p == 0, False, p == 0)
                with eng.Fori(1, NB // 2 - 1) as j:
                    for p in range(2):
                        blk(b, b * NB + j * 2 + p, j * 2 + p, p, False, False, False)
                for p in range(2):
                    blk(b, b * NB + (NB - 2 + p), NB - 2 + p, p, False, p == 1, False)
                if drain is not None:
                    drain(b)

        @block.sync
        def _(sp):
            for t, d in ((wq, Wq), (wk, Wk), (wv, Wv), (wo, Wo)):
                sp.dma_start(t[:], d).then_inc(w_in, 16)
            for i, d in enumerate((norm_w, norm_b, bq, bk, bv, bo)):
                sp.dma_start(cols[:, i:i + 1], d.rearrange("(c o) -> c o", o=1)).then_inc(w_in, 16)
            for c in range(2):
                sp.dma_start(xb[:, 0, c * N // 2:(c + 1) * N // 2], x_v[0, :, c * N // 2:(c + 1) * N // 2]).then_inc(x_in, 16)
            for b in range(B):
                if b + 1 < B:
                    sp.wait_ge(x_in, 32 * (b + 1))
                    if b >= 1:
                        sp.wait_ge(t_out, 16 * b * NB // 2)
                    for c in range(2):
                        sp.dma_start(xb[:, (b + 1) % 2, c * N // 2:(c + 1) * N // 2],
                                     x_v[b + 1, :, c * N // 2:(c + 1) * N // 2]).then_inc(x_in, 16)
                with sp.Fori(0, NB // 2) as j:
                    sp.wait_ge(t_done, (j * 2) + (b * NB + 2))
                    sp.dma_start(t_dram[:, ds(j * BANK + b * N, BANK)],
                                 xb[:, b % 2, ds(j * BANK, BANK)]).then_inc(t_out, 16)
            sp.wait_ge(t_out, 16 * B * NB // 2)

        @block.gpsimd
        def _(pool):
            nc.gpsimd.memset(ident[:], 0.0).then_inc(const_a, 1)
            nc.gpsimd.memset(gavg[:], float(GROUPS) / C).then_inc(const_a, 1)
            nc.gpsimd.memset(epsc[:], EPS).then_inc(const_b, 1)
            pool.wait_ge(const_a, 2)
            nc.gpsimd.affine_select(out=ident[:], in_=ident[:], compare_op=ALU.not_equal, fill=1.0, base=0,
                                    pattern=[[-1, C]], channel_multiplier=1).then_inc(const_b, 1)
            per = C // GROUPS
            gv = gavg[:].rearrange("p (g c) -> p g c", c=per)
            nc.gpsimd.affine_select(out=gv, in_=gv, compare_op=ALU.is_ge, fill=0.0, base=0,
                                    pattern=[[-per, GROUPS], [0, per]], channel_multiplier=1).then_inc(const_a, 1)
            pool.wait_ge(const_a, 3)
            nc.gpsimd.affine_select(out=gv, in_=gv, compare_op=ALU.is_ge, fill=0.0, base=per - 1,
                                    pattern=[[per, GROUPS], [0, per]], channel_multiplier=-1).then_inc(const_b, 1)

        @block.tensor
        def _(pe):
            pe.wait_ge(w_in, 160)
            pe.wait_ge(const_b, 3)
            pe.transpose(m_ps[:, 0:C], wv[:], ident[:]).then_inc(wt_pe, 1)
            pe.wait_ge(wt_cp, 1)
            pe.matmul(m_ps[:, 0:C], wvT[:], wo[:], start=True, stop=True)
            pe.matmul(m_ps[:, C:C + 1], wo[:], bvc, start=True, stop=True).then_inc(wp_pe, 1)
            pe.wait_ge(wp_cp, 2)

            def project_q(n, par, at):
                pe.matmul(m_ps[:, 0:QB], wq[:], hn[:, ds(at * QB, QB)], start=True, stop=True).then_inc(q_pe, 1)

            def scores(n, par, s, first):
                qt, kc = divmod(s, KCH)
                if s == 0:
                    pe.wait_ge(q_l, n + 1)
                if s % 2 == 0 and not (first and s < 4):
                    pe.wait_ge(sc_cp, n * GRP + (s // 2 - 1))
                dst = s_ps[:, s // 2 % 2, s % 2, :]
                qs, ks = slice(qt * C, (qt + 1) * C), slice(kc * BANK, (kc + 1) * BANK)
                pe.matmul(dst, q_hi[:, par, qs], k_hi[:, ks], start=True, stop=False)
                pe.matmul(dst, q_hi[:, par, qs], k_lo[:, ks], start=False, stop=False)
                mm = pe.matmul(dst, q_lo[:, par, qs], k_hi[:, ks], start=False, stop=True)
                if s % 2:
                    mm.then_inc(sc_pe, 1)

            def turn(n, par, s, first):
                if s % (STEPS // XCH) == 0:
                    pe.wait_ge(exp_done, n * 2 * XCH + (XCH + s // (STEPS // XCH) + 1))
                if not (first and s < 2):
                    pe.wait_ge(p_lo, n * STEPS + (s - 1))
                for k in range(2):
                    for qt in range(QT):
                        kt = 2 * s + k
                        mm = pe.transpose(pt_ps[:, s % 2, k, qt * C:(qt + 1) * C],
                                          s_sb[:, par, qt, kt * C:(kt + 1) * C], ident[:])
                mm.then_inc(tr_pe, 1)

            def weigh(n, s, first):
                pe.wait_ge(p_lo, n * STEPS + (s + 1))
                if s == 0 and not first:
                    pe.wait_ge(on_done, n)
                o = o_ps[:, 0:QB]
                for k in range(2):
                    kt = 2 * s + k
                    pe.matmul(o, v_hi[:, kt, :], pt_hi[:, s % 2, k, :], start=(kt == 0), stop=False)
                    pe.matmul(o, v_lo[:, kt, :], pt_hi[:, s % 2, k, :], start=False, stop=False)
                    mm = pe.matmul(o, v_hi[:, kt, :], pt_lo[:, s % 2, k, :], start=False, stop=(kt == KT - 1))
                mm.then_inc(pv_pe, 1)

            def image(b):
                pe.wait_ge(gn_step, b * 4 + 1)
                pe.matmul(m_ps[:, 0:2], gavg[:], mom[:], start=True, stop=True).then_inc(gn_pe, 1)
                pe.wait_ge(h_done, b * XCH + 1)
                pe.wait_ge(gn_step, b * 4 + 2)
                for m in range(2):
                    if m == 1:
                        pe.wait_ge(q_l, b * NB + 1)
                    project_q(None, m, m)
                for g in range(KV):
                    if g < KCH and g % 2 == 0:
                        pe.wait_ge(h_done, b * XCH + (g // 2 + 1))
                    if g >= 4:
                        pe.wait_ge(kv_lo, b * KV + (g - 3))
                    dst = s_ps[:, g // 2 % 2, g % 2, :]
                    if g < KCH:
                        mm = pe.matmul(dst, wk[:], hn[:, g * BANK:(g + 1) * BANK], start=True, stop=True)
                    else:
                        for i in range(4):
                            kt = (g - KCH) * 4 + i
                            mm = pe.matmul(dst[:, i * C:(i + 1) * C], hn[:, kt * C:(kt + 1) * C], wvo[:],
                                           start=True, stop=True)
                    mm.then_inc(kv_pe, 1)
                pe.wait_ge(kv_lo, b * KV + KV)
                for s in range(2 * KCH):
                    scores(b * NB, 0, s, True)

            def blk(b, n, at, p, first, last, skip):
                for s in range(AHEAD):
                    if not last:
                        scores(n + 1, 1 - p, s, False)
                for s in range(STEPS):
                    turn(n, p, s, first)
                    if not last and s + AHEAD < STEPS:
                        scores(n + 1, 1 - p, s + AHEAD, False)
                    if s:
                        weigh(n, s - 1, first)
                    elif not first:
                        weigh(n - 1, STEPS - 1, False)
                    if s == 4 and not (isinstance(at, int) and at >= NB - 2):
                        if not first:
                            pe.wait_ge(rb_cp, n)
                        else:
                            pe.wait_ge(q_l, n + 2)
                        project_q(n + 2, p, at + 2)
                    if s == 9:
                        if not (isinstance(at, int) and at >= NB - 2):
                            pe.wait_ge(q_l, n + 3)
                        pe.wait_ge(inv_done, n + 1)
                        for qt in range(QT):
                            mm = pe.matmul(m_ps[:, qt * C:(qt + 1) * C],
                                           rinv[:, p, qt:qt + 1].to_broadcast([C, C]), ident[:],
                                           start=True, stop=True)
                        mm.then_inc(rb_pe, 1)
                if last:
                    weigh(n, STEPS - 1, False)

            walk(pe, image, blk)

        @block.scalar
        def _(act):
            nc.scalar.preload_act_table_set("natural_log_exp_and_others")
            act.wait_ge(wt_pe, 1)
            nc.scalar.copy(wvT[:], m_ps[:, 0:C]).then_inc(wt_cp, 1)
            act.wait_ge(wp_pe, 1)
            nc.scalar.copy(wvo[:], m_ps[:, 0:C]).then_inc(wp_cp, 1)

            def split_q(n, par):
                act.wait_ge(q_pe, n + 1)
                nc.scalar.activation(q_hi[:, par, :], m_ps[:, 0:QB], ACT.Identity, bias=bqc).then_inc(q_h, 1)

            def exps(n, par, qt, c):
                if c == 0:
                    act.wait_ge(mx_done, n * QT + (qt + 1))
                sl = s_sb[:, par, qt, c * XW:(c + 1) * XW]
                nc.scalar.activation(sl, sl, ACT.Exp, bias=nmax[:, par, qt:qt + 1],
                                     accum_out=rsum[:, par, qt, c:c + 1]).then_inc(exp_done, 1)

            def image(b):
                act.wait_ge(gn_step, b * 4 + 3)
                nc.scalar.activation(gst[:, 4:5], gst[:, 3:4], ACT.Ln, bias=epsc[:]).then_inc(gn_ln, 1)
                act.wait_ge(gn_ln, b + 1)
                nc.scalar.activation(gst[:, 5:6], gst[:, 4:5], ACT.Exp, scale=-0.5).then_inc(gn_rs, 1)
                act.wait_ge(gn_step, b * 4 + 4)
                for c in range(XCH):
                    nc.scalar.activation(hn[:, c * XW:(c + 1) * XW], xb[:, ds((b % 2), 1), c * XW:(c + 1) * XW],
                                         ACT.Identity, bias=gb[:], scale=ga[:]).then_inc(h_done, 1)
                    if c == 0:
                        split_q(b * NB, 0)
                        split_q(b * NB + 1, 1)
                for g in range(KV):
                    act.wait_ge(kv_pe, b * KV + (g + 1))
                    src = s_ps[:, g // 2 % 2, g % 2, :]
                    if g < KCH:
                        nc.scalar.activation(k_hi[:, g * BANK:(g + 1) * BANK], src, ACT.Identity,
                                             bias=bkc).then_inc(kv_hi, 1)
                    else:
                        t0 = (g - KCH) * 4
                        nc.scalar.copy(v_hi[:, t0:t0 + 4, :], src).then_inc(kv_hi, 1)
                for c in range(XCH):
                    exps(b * NB, 0, 0, c)

            def blk(b, n, at, p, first, last, skip):
                exps(n, p, 1, 0)
                for s in range(STEPS):
                    act.wait_ge(tr_pe, n * STEPS + (s + 1))
                    if not (first and s < 2):
                        act.wait_ge(pv_pe, n * STEPS + (s - 1))
                    nc.scalar.copy(pt_hi[:, s % 2, :, :], pt_ps[:, s % 2, :, :]).then_inc(p_hi, 1)
                    if s in (0, 2, 4):
                        exps(n, p, 1, s // 2 + 1)
                    if s in (7, 9, 11, 13) and not last:
                        exps(n + 1, 1 - p, 0, (s - 7) // 2)
                    if s == 5 and not (isinstance(at, int) and at >= NB - 2):
                        split_q(n + 2, p)
                    if s == 10:
                        act.wait_ge(rb_pe, n + 1)
                        if not first:
                            act.wait_ge(on_done, n)
                        nc.scalar.copy(rb_sb[:], m_ps[:, 0:QB]).then_inc(rb_cp, 1)

            walk(act, image, blk)

        @block.vector
        def _(dve):
            dve.wait_ge(wp_pe, 1)
            dve.wait_ge(wp_cp, 1)
            nc.vector.tensor_tensor(bvo[:], m_ps[:, C:C + 1], boc, ALU.add).then_inc(wp_cp, 1)

            def split_q(n, par):
                dve.wait_ge(q_h, n + 1)
                nc.vector.scalar_tensor_tensor(out=q_lo[:, par, :], in0=m_ps[:, 0:QB], scalar=bqc,
                                               in1=q_hi[:, par, :].bitcast(F32), op0=ALU.add,
                                               op1=ALU.subtract).then_inc(q_l, 1)

            def score_group(n, par, g, first):
                qt, gi = divmod(g, GRP // QT)
                dve.wait_ge(sc_pe, n * GRP + (g + 1))
                if g == 0 and not first:
                    dve.wait_ge(tr_pe, n * STEPS - STEPS)
                nc.vector.tensor_scalar(s_sb[:, par, qt, gi * 2 * BANK:(gi + 1) * 2 * BANK],
                                        s_ps[:, g % 2, :, :], SCALE, None, ALU.mult, ALU.max,
                                        accum_out=mx[:, par, qt, gi:gi + 1]).then_inc(sc_cp, 1)
                if gi == GRP // QT - 1:
                    dve.wait_ge(sc_cp, n * GRP + (g + 1))
                    nc.vector.tensor_reduce(nmax[:, par, qt:qt + 1], mx[:, par, qt, :], AX.X, ALU.max,
                                            negate=True).then_inc(mx_done, 1)

            def finish(n, at, par, bpar):
                dve.wait_ge(pv_pe, n * STEPS + STEPS)
                dve.wait_ge(rb_cp, n + 1)
                nc.vector.tensor_tensor(on[:], o_ps[:, 0:QB], rb_sb[:], ALU.mult).then_inc(on_done, 1)
                dve.wait_ge(on_done, n + 1)
                xs = xb[:, ds(bpar, 1), ds(at * QB, QB)].rearrange("c o n -> c (o n)")
                nc.vector.scalar_tensor_tensor(out=xs, in0=on[:], scalar=bvo[:], in1=xs, op0=ALU.add,
                                               op1=ALU.add).then_inc(t_done, 1)

            def image(b):
                dve.wait_ge(x_in, b * 32 + 32)
                for c in range(KCH):
                    nc.vector.bn_stats(bn[:, c, :], xb[:, ds((b % 2), 1), c * BANK:(c + 1) * BANK]).then_inc(bn_done, 1)
                dve.wait_ge(bn_done, b * (KCH + 3) + KCH)
                nc.vector.memset(gst[:, 6:7], 0.0)
                nc.vector.bn_aggr(mom[:], bn[:].rearrange("p a s -> p (a s)")).then_inc(bn_done, 1)
                dve.wait_ge(bn_done, b * (KCH + 3) + (KCH + 1))
                nc.vector.tensor_tensor(gtmp[:], mom[:, 0:1], mom[:, 0:1], ALU.mult).then_inc(bn_done, 1)
                dve.wait_ge(bn_done, b * (KCH + 3) + (KCH + 2))
                nc.vector.tensor_tensor(mom[:, 1:2], mom[:, 1:2], gtmp[:], ALU.add).then_inc(gn_step, 1)
                dve.wait_ge(gn_pe, b + 1)
                nc.vector.tensor_copy(gst[:, 0:2], m_ps[:, 0:2]).then_inc(gn_step, 1)
                dve.wait_ge(gn_step, b * 4 + 2)
                nc.vector.scalar_tensor_tensor(out=gst[:, 2:3], in0=gst[:, 0:1], scalar=gst[:, 0:1],
                                               in1=gst[:, 1:2], op0=ALU.mult, op1=ALU.subtract).then_inc(den_done, 1)
                dve.wait_ge(den_done, b * (NB + 2) + 1)
                nc.vector.tensor_scalar(gst[:, 3:4], gst[:, 2:3], -1.0, 0.0, ALU.mult, ALU.max).then_inc(gn_step, 1)
                dve.wait_ge(gn_rs, b + 1)
                nc.vector.tensor_tensor(ga[:], gst[:, 5:6], gnw, ALU.mult).then_inc(den_done, 1)
                dve.wait_ge(den_done, b * (NB + 2) + 2)
                nc.vector.tensor_tensor(gtmp[:], gst[:, 0:1], ga[:], ALU.mult).then_inc(bn_done, 1)
                dve.wait_ge(bn_done, b * (KCH + 3) + (KCH + 3))
                nc.vector.tensor_tensor(gb[:], gnb, gtmp[:], ALU.subtract).then_inc(gn_step, 1)
                split_q(b * NB, 0)
                split_q(b * NB + 1, 1)
                for g in range(KV):
                    dve.wait_ge(kv_hi, b * KV + (g + 1))
                    src = s_ps[:, g // 2 % 2, g % 2, :]
                    if g < KCH:
                        sl = slice(g * BANK, (g + 1) * BANK)
                        nc.vector.scalar_tensor_tensor(out=k_lo[:, sl], in0=src, scalar=bkc,
                                                       in1=k_hi[:, sl].bitcast(F32), op0=ALU.add,
                                                       op1=ALU.subtract).then_inc(kv_lo, 1)
                    else:
                        t0 = (g - KCH) * 4
                        nc.vector.tensor_tensor(v_lo[:, t0:t0 + 4, :].rearrange("p a c -> p (a c)"), src,
                                                v_hi[:, t0:t0 + 4, :].rearrange("p a c -> p (a c)").bitcast(F32),
                                                ALU.subtract).then_inc(kv_lo, 1)
                for g in range(GRP):
                    score_group(b * NB, 0, g, True)

            def blk(b, n, at, p, first, last, skip):
                for s in range(STEPS):
                    dve.wait_ge(p_hi, n * STEPS + (s + 1))
                    nc.vector.tensor_tensor(pt_lo[:, s % 2, :, :], pt_ps[:, s % 2, :, :],
                                            pt_hi[:, s % 2, :, :].bitcast(F32), ALU.subtract).then_inc(p_lo, 1)
                    if s == 1 and not first:
                        finish(n - 1, at - 1, 1 - p, b % 2)
                    if s == 6 and not (isinstance(at, int) and at >= NB - 2):
                        split_q(n + 2, p)
                    if s == 7:
                        dve.wait_ge(exp_done, n * 2 * XCH + 2 * XCH)
                        nc.vector.tensor_reduce(rden[:, p, :], rsum[:, p, :, :], AX.X, ALU.add).then_inc(den_done, 1)
                        dve.wait_ge(den_done, b * (NB + 2) + (at + 3))
                        nc.vector.reciprocal(rinv[:, p, :], rden[:, p, :]).then_inc(inv_done, 1)
                    if not last:
                        for g in range(GRP):
                            if max(0, 2 * g + 2 - AHEAD) == s:
                                score_group(n + 1, 1 - p, g, n_first(at))
                if last:
                    finish(n, at, p, b % 2)

            def n_first(at):
                return isinstance(at, int) and at == 0

            walk(dve, image, blk)


def scan_attention_and_experts(nc, t_dram, W_kv, q_proj, router_w, router_b, expert_w, expert_b, out):
    B, _, H, W = out.shape
    N = H * W
    HEADS = q_proj.shape[0]
    E = router_w.shape[1]
    TOK = BANK
    PER = N // TOK
    NBLK = B * PER
    TT = TOK // C
    QUAD, HALF = 32, 16
    LOWEST = -3.0e38
    out_v = out.rearrange("b c h w -> b c (h w)")

    with ExitStack() as ctx:
        def sb(name, shape, dt=F32):
            return ctx.enter_context(nc.sbuf_tensor(name, shape, dt))

        def psum(name, shape):
            return ctx.enter_context(nc.psum_tensor(name, shape, F32))

        def sem(name):
            return ctx.enter_context(nc.semaphore(name))

        t = sb("t", [C, NBLK * TOK])
        wkv = sb("wkv", [C, HEADS, 2, C])
        w_hi, w_lo = sb("w_hi", [C, HEADS, 2, C], F32R), sb("w_lo", [C, HEADS, 2, C], F32R)
        qcol = sb("qcol", [C, HEADS])
        qz = sb("qz", [C, HEADS, QUAD])
        rw = sb("rw", [C, E])
        rbias = sb("rbias", [C, E])
        ew = sb("ew", [C, E, C])
        eb = sb("eb", [C, C])
        eb_hi, eb_lo = sb("eb_hi", [C, C], F32R), sb("eb_lo", [C, C], F32R)
        ident, center, mean_w = sb("ident1", [C, C]), sb("center", [C, C]), sb("mean_w", [C, C])
        sel_h = sb("sel_h", [C, HEADS, C], F32R)
        sel_e = sb("sel_e", [C, E, C], F32R)
        low_rows4, low_rows = sb("low_rows4", [C, 4]), sb("low_rows", [C, 1])
        before = sb("before", [C, E, E])
        place_i = sb("place_i", [C, E])
        zeros = sb("zeros", [C, TOK])
        epsc = sb("epsc1", [C, 1])

        ln_sq, ln_l, ln_r = sb("ln_sq", [C, TOK]), sb("ln_l", [C, TOK]), sb("ln_r", [C, TOK])
        xf = sb("xf", [C, TOK])
        xn_hi, xn_lo = sb("xn_hi", [C, 2, TOK], F32R), sb("xn_lo", [C, 2, TOK], F32R)
        xn2 = sb("xn2", [C, 2, TOK])
        sk = sb("sk", [C, HEADS, TOK])
        sv = sb("sv", [C, 3, TOK])
        m_r, d_r, e_r, u_r = (sb(n, [C, TOK]) for n in ("m_r", "d_r", "e_r", "u_r"))
        l_r, b_r, a_r = (sb(n, [C, TOK]) for n in ("l_r", "b_r", "a_r"))
        zr = sb("zr", [C, 2, TOK], F32R)
        new_w, old_w = sb("new_w", [C, TOK], F32R), sb("old_w", [C, TOK], F32R)
        z = sb("z", [C, 2, TOK])
        y = sb("y", [C, HEADS, TOK])
        acc = sb("acc", [C, TOK])
        xg = sb("xg", [C, 3, TOK])
        lg = sb("lg", [C, TT, E])
        ge, gel = sb("ge", [C, TT, E, E]), sb("gel", [C, TT, E, E])
        r1, r2, rank, pick = (sb(n, [C, TT, E]) for n in ("r1", "r2", "rank", "pick"))
        sl, dl, th, g1, g2 = (sb(n, [C, TT, E]) for n in ("sl", "dl", "th", "g1", "g2"))
        ssum = sb("ssum", [C, TT])
        ghr = sb("ghr", [C, TT, E], F32R)
        g16 = sb("g16", [C, TT, 2 * E])
        gt = sb("gt", [C, TOK], F32R)

        kv_ps = psum("kv_ps", [C, 2, BANK])
        bc_ps = psum("bc_ps", [C, 2, BANK])
        row_ps = psum("row_ps", [C, BANK])
        mo_ps = psum("mo_ps", [C, BANK])
        lnd_ps = psum("lnd_ps", [C, BANK])
        lnv_ps = psum("lnv_ps", [C, BANK])

        names = """w_in t_in t_out cst1 cst2 cst3 wt_pe wt_hi wt_lo
            k_pe s_pe v_pe bc_pe g_pe x_pe c1_pe w1_pe c2_pe w2_pe r_pe gt_pe
            k_act v_act sq1 sq2 ln1 ln2 rs1 rs2 hi_act e_act lu_act b_act th_act gt_act
            z_dve y_dve m_dve d_dve u_dve l_dve rows_dve xf_dve lo_dve xn2_dve xg_dve t2_dve out_dve gate g16_dve
            acc_pool""".split()
        (w_in, t_in, t_out, cst1, cst2, cst3, wt_pe, wt_hi, wt_lo,
         k_pe, s_pe, v_pe, bc_pe, g_pe, x_pe, c1_pe, w1_pe, c2_pe, w2_pe, r_pe, gt_pe,
         k_act, v_act, sq1, sq2, ln1, ln2, rs1, rs2, hi_act, e_act, lu_act, b_act, th_act, gt_act,
         z_dve, y_dve, m_dve, d_dve, u_dve, l_dve, rows_dve, xf_dve, lo_dve, xn2_dve, xg_dve, t2_dve, out_dve,
         gate, g16_dve, acc_pool) = (sem(n) for n in names)
        GATE = 12
        ROWS = 5

        block = ctx.enter_context(nc.Block())

        def at_least(eng, s, value):
            if not (isinstance(value, int) and value <= 0):
                eng.wait_ge(s, value)

        def walk(eng, it):
            def pair(n, first, last=False):
                for p in range(2):
                    it(n + p, p, keys=True, values=not (isinstance(n, int) and n + p < 1),
                       experts=not (isinstance(n, int) and n + p < 2), norm=not (last and p == 1),
                       new_rows=first and p == 0, new_values=first and p == 1)

            pair(0, True)
            with eng.Fori(1, PER // 2) as j:
                pair(j * 2, False)
            with eng.Fori(1, B - 1) as b:
                pair(b * PER, True)
                with eng.Fori(1, PER // 2) as j:
                    pair(b * PER + j * 2, False)
            pair((B - 1) * PER, True)
            with eng.Fori(1, PER // 2 - 1) as j:
                pair(j * 2 + (B - 1) * PER, False)
            pair(NBLK - 2, False, True)
            it(NBLK, 0, keys=False, values=True, experts=True, norm=False, new_rows=False, new_values=False)
            it(NBLK + 1, 1, keys=False, values=False, experts=True, norm=False, new_rows=False, new_values=False)

        def tok(n):
            return slice(n * TOK, (n + 1) * TOK) if isinstance(n, int) else ds(n * TOK, TOK)

        @block.sync
        def _(sp):
            sp.dma_start(wkv[:], W_kv.rearrange("(h d two) c -> d h two c", h=HEADS, two=2)).then_inc(w_in, 16)
            sp.dma_start(qcol[:], q_proj.rearrange("h d -> d h"), allow_slow_non_contiguous=True).then_inc(w_in, 16)
            sp.dma_start(rw[:], router_w).then_inc(w_in, 16)
            sp.dma_start(rbias[:], router_b.rearrange("(o e) -> o e", o=1).to_broadcast([C, E])).then_inc(w_in, 16)
            sp.dma_start(ew[:], expert_w.rearrange("e c d -> c e d")).then_inc(w_in, 16)
            sp.wait_ge(cst2, 1)
            for i in range(2):
                sp.dma_start(eb[i * E:(i + 1) * E, :], expert_b).then_inc(w_in, 16)
            for b in range(B):
                if b:
                    sp.wait_ge(t_in, 16 * b)
                sp.dma_start(t[:, b * N:(b + 1) * N], t_dram[:, b * N:(b + 1) * N]).then_inc(t_in, 16)
            for b in range(B):
                with sp.Fori(0, PER) as j:
                    sp.wait_ge(out_dve, j + (b * PER + 1))
                    sp.dma_start(out_v[b, :, ds(j * TOK, TOK)], t[:, ds(j * TOK + b * N, TOK)]).then_inc(t_out, 16)
            sp.wait_ge(t_out, 16 * NBLK)

        @block.gpsimd
        def _(pool):
            nc.gpsimd.memset(eb[:], 0.0).then_inc(cst2, 1)
            nc.gpsimd.memset(ident[:], 0.0).then_inc(cst1, 1)
            nc.gpsimd.memset(low_rows4[:], 1.0).then_inc(cst1, 1)
            nc.gpsimd.memset(before[:], 1.0).then_inc(cst1, 1)
            nc.gpsimd.memset(mean_w[:], 1.0 / C).then_inc(cst1, 1)
            nc.gpsimd.memset(epsc[:], EPS).then_inc(cst1, 1)
            nc.gpsimd.memset(zeros[:], 0.0).then_inc(cst1, 1)
            nc.gpsimd.memset(qz[:], 0.0).then_inc(cst1, 1)
            nc.gpsimd.memset(gt[:].bitcast(F32), 0.0).then_inc(cst1, 1)
            pool.wait_ge(cst1, 8)
            nc.gpsimd.affine_select(out=ident[:], in_=ident[:], compare_op=ALU.not_equal, fill=1.0, base=0,
                                    pattern=[[-1, C]], channel_multiplier=1).then_inc(cst3, 1)
            nc.gpsimd.affine_select(out=before[:], in_=before[:], compare_op=ALU.is_gt, fill=0.0, base=0,
                                    pattern=[[1, E], [-1, E]], channel_multiplier=0).then_inc(cst3, 1)
            nc.gpsimd.affine_select(out=low_rows4[:], in_=low_rows4[:], compare_op=ALU.is_ge, fill=0.0, base=-HALF,
                                    pattern=[[-QUAD, 4]], channel_multiplier=1).then_inc(cst1, 1)
            pool.wait_ge(cst1, 9)
            nc.gpsimd.affine_select(out=low_rows4[:], in_=low_rows4[:], compare_op=ALU.is_ge, fill=0.0,
                                    base=QUAD - 1, pattern=[[QUAD, 4]], channel_multiplier=-1).then_inc(cst3, 1)

            def it(n, p, keys, values, experts, norm, new_rows, new_values):
                if not values:
                    return
                v = n - 1
                at_least(pool, t2_dve, v)
                for h in range(1, HEADS):
                    pool.wait_ge(y_dve, v * HEADS + (h + 1))
                    if h > 1:
                        pool.wait_ge(acc_pool, v * (HEADS - 1) + (h - 1))
                    nc.gpsimd.tensor_tensor(acc[:], y[:, 0, :] if h == 1 else acc[:], y[:, h, :],
                                            ALU.add).then_inc(acc_pool, 1)

            walk(pool, it)

        @block.tensor
        def _(pe):
            pe.wait_ge(w_in, 16 * 7)
            pe.wait_ge(cst3, 5)
            for g in range(2 * HEADS // TT):
                if g >= 2:
                    pe.wait_ge(wt_lo, g - 1)
                for i in range(TT):
                    h, two = divmod(g * TT + i, 2)
                    mm = pe.transpose(kv_ps[:, g % 2, i * C:(i + 1) * C], wkv[:, h, two, :], ident[:])
                mm.then_inc(wt_pe, 1)
            pe.wait_ge(wt_lo, 2 * HEADS // TT)

            def project(dst, head, two, par):
                pe.matmul(dst, w_hi[:, head, two, :], xn_hi[:, par, :], start=True, stop=False)
                pe.matmul(dst, w_hi[:, head, two, :], xn_lo[:, par, :], start=False, stop=False)
                return pe.matmul(dst, w_lo[:, head, two, :], xn_hi[:, par, :], start=False, stop=True)

            def row_sums(n, j):
                if j == 0:
                    at_least(pe, d_dve, n)
                pe.wait_ge(k_act, n * HEADS + (4 * j + 4))
                for g in range(4):
                    h = 4 * j + g
                    mm = pe.matmul(row_ps[QUAD * g:QUAD * (g + 1), :], qz[:, h, :], sk[:, h, :],
                                   start=(j == 0), stop=(j == 1))
                if j == 1:
                    mm.then_inc(s_pe, 1)

            def norm_center(n, s_in, free, s_out):
                if s_in is not None:
                    pe.wait_ge(s_in, n + 1)
                at_least(pe, *free)
                pe.matmul(lnd_ps[:], center[:], t[:, tok(n)], start=True, stop=True).then_inc(s_out, 1)

            def norm_var(n, sq, free, s_out):
                pe.wait_ge(sq, n + 1)
                at_least(pe, *free)
                pe.matmul(lnv_ps[:], mean_w[:], ln_sq[:], start=True, stop=True).then_inc(s_out, 1)

            pe.wait_ge(t_in, 16)
            norm_center(0, None, (xn2_dve, 0), c1_pe)
            norm_var(0, sq1, (gt_act, 0), w1_pe)

            def it(n, p, keys, values, experts, norm, new_rows, new_values):
                v, q = n - 1, n - 2
                if keys:
                    pe.wait_ge(lo_dve, n + 1)
                    for h in range(HEADS):
                        if h == 0:
                            at_least(pe, v_act, (n - 1) * HEADS)
                        if h >= 2:
                            pe.wait_ge(k_act, n * HEADS + (h - 1))
                        project(kv_ps[:, h % 2, :], h, 0, p).then_inc(k_pe, 1)
                        if h == 1 and experts:
                            router(q, p)
                        if h == 5:
                            row_sums(n, 0)
                elif experts:
                    router(q, p)
                if values:
                    for h in range(HEADS):
                        if h < 2 and keys:
                            pe.wait_ge(k_act, n * HEADS + (HEADS - 1 + h))
                        elif h < 2:
                            pe.wait_ge(v_act, v * HEADS)
                        else:
                            pe.wait_ge(v_act, v * HEADS + (h - 1))
                        project(kv_ps[:, h % 2, :], h, 1, 1 - p).then_inc(v_pe, 1)
                        if h == 0:
                            pe.wait_ge(rows_dve, v * ROWS + ROWS)
                        else:
                            pe.wait_ge(z_dve, v * HEADS + h)
                        pe.matmul(bc_ps[:, 0, :], sel_h[:, h, :], new_w[:], start=True, stop=True)
                        if h:
                            pe.wait_ge(y_dve, v * HEADS + h)
                        pe.matmul(bc_ps[:, 1, :], sel_h[:, h, :], old_w[:], start=True, stop=True).then_inc(bc_pe, 1)
                        if h == 1 and keys:
                            row_sums(n, 1)
                        if h == 3 and experts:
                            turn_gates(q)
                elif keys:
                    row_sums(n, 1)
                if not values and experts:
                    turn_gates(q)
                if experts:
                    pe.wait_ge(gt_act, q + 1)
                    if not values:
                        pe.wait_ge(out_dve, q)
                    pe.matmul(mo_ps[:], eb_hi[:], gt[:], start=True, stop=False)
                    pe.matmul(mo_ps[:], eb_lo[:], gt[:], start=False, stop=False)
                    if values:
                        pe.wait_ge(y_dve, v * HEADS + HEADS)
                    spread(q, 0)
                    spread(q, 1)
                for e in range(E):
                    if experts:
                        pe.wait_ge(xg_dve, q * E + (e + 1))
                        if e + 2 < E:
                            spread(q, e + 2)
                        pe.matmul(mo_ps[:], ew[:, e, :], xg[:, e % 3, :], start=False,
                                  stop=(e == E - 1)).then_inc(x_pe, 1)
                    if norm and e == 0:
                        if n_is(n, 0) or not isinstance(n, int) or n % PER == PER - 1:
                            pe.wait_ge(t_in, norm_image(n))
                        norm_center(n + 1, None, (xn2_dve, n - 1), c1_pe)
                    if norm and e == 2:
                        norm_var(n + 1, sq1, (gt_act, n - 1), w1_pe)
                    if values and e == 4:
                        if norm:
                            norm_center(v, t2_dve, (xf_dve, n + 2), c2_pe)
                        else:
                            norm_center(v, t2_dve, (xn2_dve, v), c2_pe)
                    if values and e == 6:
                        norm_var(v, sq2, (ln1, n + 2 if norm else NBLK), w2_pe)

            def n_is(n, k):
                return isinstance(n, int) and n == k

            def norm_image(n):
                return 16 * (1 if isinstance(n, int) and n + 1 < PER else B)

            def spread(q, e):
                if e >= 2:
                    pass
                pe.matmul(bc_ps[:, e % 2, :], sel_e[:, e, :], gt[:], start=True, stop=True).then_inc(g_pe, 1)

            def router(q, p):
                pe.wait_ge(xn2_dve, q + 1)
                for i in range(TT):
                    mm = pe.matmul(lnv_ps[:, i * E:(i + 1) * E], xn2[:, p, i * C:(i + 1) * C], rw[:],
                                   start=True, stop=True)
                mm.then_inc(r_pe, 1)

            def turn_gates(q):
                pe.wait_ge(g16_dve, 2 * q + 2)
                for i in range(TT):
                    mm = pe.transpose(lnv_ps[0:2 * E, i * C:(i + 1) * C], g16[:, i, :], ident[:])
                mm.then_inc(gt_pe, 1)

            walk(pe, it)

        @block.scalar
        def _(act):
            for g in range(2 * HEADS // TT):
                act.wait_ge(wt_pe, g + 1)
                dst = w_hi[:].rearrange("p h w c -> p (h w c)")[:, g * BANK:(g + 1) * BANK]
                nc.scalar.copy(dst, kv_ps[:, g % 2, :]).then_inc(wt_hi, 1)

            def norm_pre(n, c_pe, free, sq):
                act.wait_ge(c_pe, n + 1)
                at_least(act, *free)
                nc.scalar.activation(ln_sq[:], lnd_ps[:], ACT.Square).then_inc(sq, 1)

            def norm_post(n, w_pe, free, ln, rs):
                act.wait_ge(w_pe, n + 1)
                nc.scalar.activation(ln_l[:], lnv_ps[:], ACT.Ln, bias=epsc[:]).then_inc(ln, 1)
                act.wait_ge(ln, n + 1)
                at_least(act, *free)
                nc.scalar.activation(ln_r[:], ln_l[:], ACT.Exp, scale=-0.5).then_inc(rs, 1)

            def high(n, par):
                act.wait_ge(xf_dve, n + 1)
                at_least(act, v_pe, (n - 1) * HEADS)
                nc.scalar.copy(xn_hi[:, par, :], xf[:]).then_inc(hi_act, 1)

            nc.scalar.preload_act_table_set("natural_log_exp_and_others")
            act.wait_ge(cst3, 3)
            norm_pre(0, c1_pe, (w2_pe, 0), sq1)
            norm_post(0, w1_pe, (xn2_dve, 0), ln1, rs1)
            high(0, 0)

            def it(n, p, keys, values, experts, norm, new_rows, new_values):
                v, q = n - 1, n - 2

                def gates():
                    act.wait_ge(gate, q * GATE + 9)
                    nc.scalar.activation(th[:], dl[:], ACT.Tanh).then_inc(th_act, 1)

                if keys or values:
                    nc.scalar.preload_act_table_set("silu_and_others")
                if keys:
                    at_least(act, s_pe, n)
                    for h in range(HEADS):
                        act.wait_ge(k_pe, n * HEADS + (h + 1))
                        nc.scalar.activation(sk[:, h, :], kv_ps[:, h % 2, :], ACT.Silu).then_inc(k_act, 1)
                if experts:
                    gates()
                if values:
                    for h in range(HEADS):
                        act.wait_ge(v_pe, v * HEADS + (h + 1))
                        at_least(act, z_dve, v * HEADS + (h - 2))
                        nc.scalar.activation(sv[:, h % 3, :], kv_ps[:, h % 2, :], ACT.Silu).then_inc(v_act, 1)
                        if h == 4 and experts:
                            turned(q)
                elif experts:
                    turned(q)
                nc.scalar.preload_act_table_set("natural_log_exp_and_others")
                if norm:
                    norm_pre(n + 1, c1_pe, (w2_pe, n - 1), sq1)
                if keys:
                    act.wait_ge(d_dve, n + 1)
                    nc.scalar.activation(e_r[:], d_r[:], ACT.Exp).then_inc(e_act, 1)
                if norm:
                    norm_post(n + 1, w1_pe, (xn2_dve, n - 1), ln1, rs1)
                if keys:
                    act.wait_ge(u_dve, n + 1)
                    nc.scalar.activation(l_r[:], u_r[:], ACT.Ln).then_inc(lu_act, 1)
                if norm:
                    high(n + 1, 1 - p)
                if keys:
                    act.wait_ge(l_dve, n + 1)
                    nc.scalar.activation(b_r[:], e_r[:], ACT.Exp).then_inc(b_act, 1)
                if values:
                    norm_pre(v, c2_pe, (w1_pe, n + 2 if norm else NBLK), sq2)
                    norm_post(v, w2_pe, (xf_dve, n + 2 if norm else NBLK), ln2, rs2)

            def turned(q):
                act.wait_ge(gt_pe, q + 1)
                nc.scalar.copy(gt[0:2 * E, :], lnv_ps[0:2 * E, :]).then_inc(gt_act, 1)

            walk(act, it)

        @block.vector
        def _(dve):
            dve.wait_ge(cst3, 3)
            dve.wait_ge(w_in, 16 * 7)
            nc.vector.tensor_scalar(center[:], ident[:], -1.0 / C, None, ALU.add).then_inc(cst3, 1)
            for h in range(HEADS):
                r0 = QUAD * (h % 4) + h // 4
                nc.vector.tensor_tensor(sel_h[:, h, :], ident[:, r0:r0 + 1].to_broadcast([C, C]),
                                        ident[:, r0 + HALF:r0 + HALF + 1].to_broadcast([C, C]), ALU.add)
                for col in (h // 4, h // 4 + HALF):
                    nc.vector.tensor_copy(qz[:, h, col:col + 1], qcol[:, h:h + 1])
            for e in range(E):
                nc.vector.tensor_tensor(sel_e[:, e, :], ident[:, e:e + 1].to_broadcast([C, C]),
                                        ident[:, e + E:e + E + 1].to_broadcast([C, C]), ALU.add)
            nc.vector.tensor_reduce(low_rows[:], low_rows4[:], AX.X, ALU.add).then_inc(cst2, 1)
            nc.vector.tensor_reduce(place_i[:], before[:], AX.X, ALU.add).then_inc(cst2, 1)
            nc.vector.tensor_copy(eb_hi[:], eb[:]).then_inc(cst2, 1)
            dve.wait_ge(cst2, 4)
            nc.vector.tensor_scalar(place_i[:], place_i[:], -5.0, None, ALU.add).then_inc(cst2, 1)
            nc.vector.tensor_tensor(eb_lo[:], eb[:], eb_hi[:].bitcast(F32), ALU.subtract).then_inc(cst3, 1)
            for g in range(2 * HEADS // TT):
                dve.wait_ge(wt_hi, g + 1)
                sl_ = slice(g * BANK, (g + 1) * BANK)
                nc.vector.tensor_tensor(w_lo[:].rearrange("p h w c -> p (h w c)")[:, sl_], kv_ps[:, g % 2, :],
                                        w_hi[:].rearrange("p h w c -> p (h w c)")[:, sl_].bitcast(F32),
                                        ALU.subtract).then_inc(wt_lo, 1)

            def norm_one(n, par):
                dve.wait_ge(rs1, n + 1)
                at_least(dve, hi_act, n)
                at_least(dve, lo_dve, n)
                nc.vector.tensor_tensor(xf[:], lnd_ps[:], ln_r[:], ALU.mult).then_inc(xf_dve, 1)

            def low(n, par):
                dve.wait_ge(hi_act, n + 1)
                nc.vector.tensor_tensor(xn_lo[:, par, :], xf[:], xn_hi[:, par, :].bitcast(F32),
                                        ALU.subtract).then_inc(lo_dve, 1)

            norm_one(0, 0)
            low(0, 0)

            def gates(q):
                k = [0]

                def step(ins):
                    k[0] += 1
                    ins.then_inc(gate, 1)
                    dve.wait_ge(gate, q * GATE + k[0])

                dve.wait_ge(r_pe, q + 1)
                rb4 = rbias[:].unsqueeze(1).to_broadcast([C, TT, E])
                step(nc.vector.tensor_tensor(lg[:], lnv_ps[:, 0:TT * E].rearrange("p (t e) -> p t e", t=TT), rb4, ALU.add))
                lj = lg[:].unsqueeze(2).to_broadcast([C, TT, E, E])
                li = lg[:].unsqueeze(3).to_broadcast([C, TT, E, E])
                step(nc.vector.tensor_tensor(ge[:], lj, li, ALU.is_ge))
                step(nc.vector.tensor_tensor(gel[:], ge[:], before[:].unsqueeze(1).to_broadcast([C, TT, E, E]), ALU.mult))
                nc.vector.tensor_reduce(r1[:], gel[:], AX.X, ALU.add).then_inc(gate, 1)
                k[0] += 1
                step(nc.vector.tensor_reduce(r2[:], gel[:].rearrange("p t i j -> p t j i"), AX.X, ALU.add))
                step(nc.vector.tensor_tensor(rank[:], r1[:], r2[:], ALU.subtract))
                step(nc.vector.tensor_tensor(pick[:], rank[:], place_i[:].unsqueeze(1).to_broadcast([C, TT, E]), ALU.is_lt))
                step(nc.vector.tensor_tensor(sl[:], pick[:], lg[:], ALU.mult))
                nc.vector.tensor_reduce(ssum[:], sl[:], AX.X, ALU.add).then_inc(g16_dve, 1)
                dve.wait_ge(g16_dve, 2 * q + 1)
                nc.vector.scalar_tensor_tensor(out=dl[:], in0=ssum[:].unsqueeze(2).to_broadcast([C, TT, E]),
                                               scalar=-0.5, in1=lg[:], op0=ALU.mult, op1=ALU.add).then_inc(gate, 1)

            def gates_end(q):
                dve.wait_ge(th_act, q + 1)
                nc.vector.tensor_scalar(g1[:], th[:], 0.5, 0.5, ALU.mult, ALU.add).then_inc(gate, 1)
                dve.wait_ge(gate, q * GATE + 10)
                nc.vector.tensor_tensor(g2[:], g1[:], pick[:], ALU.mult).then_inc(gate, 1)
                dve.wait_ge(gate, q * GATE + 11)
                nc.vector.tensor_copy(ghr[:], g2[:]).then_inc(gate, 1)
                dve.wait_ge(gate, q * GATE + 12)
                nc.vector.tensor_copy(g16[:, :, 0:E], ghr[:].bitcast(F32))
                nc.vector.tensor_tensor(g16[:, :, E:2 * E], g2[:], ghr[:].bitcast(F32), ALU.subtract).then_inc(g16_dve, 1)

            def rows_end(n):
                dve.wait_ge(b_act, n + 1)
                at_least(dve, bc_pe, n * HEADS)
                nc.vector.tensor_scalar(zr[:, 0, :], b_r[:], low_rows[:], None, ALU.mult).then_inc(rows_dve, 1)
                nc.vector.tensor_scalar(a_r[:], b_r[:], -1.0, 1.0, ALU.mult, ALU.add).then_inc(rows_dve, 1)
                dve.wait_ge(rows_dve, n * ROWS + 2)
                nc.vector.tensor_tensor(new_w[:], b_r[:], zr[:, 0, :].bitcast(F32), ALU.subtract).then_inc(rows_dve, 1)
                nc.vector.tensor_scalar(zr[:, 1, :], a_r[:], low_rows[:], None, ALU.mult).then_inc(rows_dve, 1)
                dve.wait_ge(rows_dve, n * ROWS + 4)
                nc.vector.tensor_tensor(old_w[:], a_r[:], zr[:, 1, :].bitcast(F32), ALU.subtract).then_inc(rows_dve, 1)

            def it(n, p, keys, values, experts, norm, new_rows, new_values):
                v, q = n - 1, n - 2
                if values:
                    rows_end(v)
                if experts:
                    gates(q)
                if values:
                    for h in range(HEADS):
                        dve.wait_ge(v_act, v * HEADS + (h + 1))
                        dve.wait_ge(bc_pe, v * HEADS + (h + 1))
                        at_least(dve, y_dve, v * HEADS + (h - 1))
                        nc.vector.tensor_tensor(z[:, h % 2, :], bc_ps[:, 0, :], sv[:, h % 3, :], ALU.mult).then_inc(z_dve, 1)
                        dve.wait_ge(z_dve, v * HEADS + (h + 1))
                        if h == 0:
                            at_least(dve, acc_pool, v * (HEADS - 1))
                        nc.vector.tensor_tensor_scan(y[:, h, :], bc_ps[:, 1, :], z[:, h % 2, :],
                                                     0.0 if new_values else y[:, h, TOK - 1:TOK],
                                                     ALU.mult, ALU.add).then_inc(y_dve, 1)
                        if h == 1 and experts:
                            gates_end(q)
                elif experts:
                    gates_end(q)

                def expert(e):
                    if experts:
                        dve.wait_ge(g_pe, q * E + (e + 1))
                        if e >= 3:
                            dve.wait_ge(x_pe, q * E + (e - 2))
                        nc.vector.tensor_tensor(xg[:, e % 3, :], bc_ps[:, e % 2, :], xn2[:, p, :], ALU.mult).then_inc(xg_dve, 1)

                expert(0)
                if keys:
                    dve.wait_ge(s_pe, n + 1)
                    at_least(dve, m_dve, n)
                    nc.vector.tensor_tensor_scan(m_r[:], row_ps[:], zeros[:],
                                                 LOWEST if new_rows else m_r[:, TOK - 1:TOK],
                                                 ALU.max, ALU.add).then_inc(m_dve, 1)
                    dve.wait_ge(m_dve, n + 1)
                    at_least(dve, l_dve, n)
                    nc.vector.tensor_tensor(d_r[:], row_ps[:], m_r[:], ALU.subtract).then_inc(d_dve, 1)
                expert(1)
                expert(2)
                if values:
                    dve.wait_ge(acc_pool, v * (HEADS - 1) + (HEADS - 1))
                    tv = t[:, tok(v)]
                    nc.vector.scalar_tensor_tensor(out=tv, in0=acc[:], scalar=1.0 / HEADS, in1=tv, op0=ALU.mult,
                                                   op1=ALU.add).then_inc(t2_dve, 1)
                if keys:
                    dve.wait_ge(e_act, n + 1)
                    at_least(dve, u_dve, n)
                    nc.vector.tensor_tensor_scan(u_r[:], e_r[:], zeros[:], 0.0 if new_rows else u_r[:, TOK - 1:TOK],
                                                 ALU.add, ALU.add).then_inc(u_dve, 1)
                expert(3)
                if norm:
                    norm_one(n + 1, 1 - p)
                expert(4)
                if keys:
                    dve.wait_ge(lu_act, n + 1)
                    nc.vector.tensor_tensor(e_r[:], d_r[:], l_r[:], ALU.subtract).then_inc(l_dve, 1)
                if norm:
                    low(n + 1, 1 - p)
                expert(5)
                expert(6)
                expert(7)
                if values:
                    dve.wait_ge(rs2, v + 1)
                    nc.vector.tensor_tensor(xn2[:, 1 - p, :], lnd_ps[:], ln_r[:], ALU.mult).then_inc(xn2_dve, 1)
                if experts:
                    dve.wait_ge(x_pe, q * E + E)
                    tq = t[:, tok(q)]
                    nc.vector.tensor_tensor(tq, mo_ps[:], tq, ALU.add).then_inc(out_dve, 1)

            walk(dve, it)


def hybrid_layers(nc, x, norm_w, norm_b, Wq, bq, Wk, bk, Wv, bv, Wo, bo, W_kv, q_proj, router_w, router_b,
                  expert_w, expert_b, out):
    B, _, H, W = x.shape
    t_dram = nc.dram_tensor("tokens", (C, B * H * W), F32, kind="Internal").ap()
    softmax_attention(nc, x, norm_w, norm_b, Wq, bq, Wk, bk, Wv, bv, Wo, bo, t_dram)
    scan_attention_and_experts(nc, t_dram, W_kv, q_proj, router_w, router_b, expert_w, expert_b, out)


_INS = ['x', 'L0_conv_norm_w', 'L0_conv_norm_b', 'L0_conv_Wq', 'L0_conv_bq', 'L0_conv_Wk', 'L0_conv_bk',
        'L0_conv_Wv', 'L0_conv_bv', 'L0_conv_Wo', 'L0_conv_bo', 'L1_attn_W_kv', 'L1_attn_q_proj',
        'L1_ffn_router_w', 'L1_ffn_router_b', 'L1_ffn_expert_w', 'L1_ffn_expert_b']
_OUTS = [((4, 128, 64, 64), 'float32')]


def kernel(**inputs):
    import numpy as _np
    import concourse.bacc as _bacc
    from concourse import mybir as _mybir
    from concourse.bass_utils import run_bass_kernel_spmd as _run

    nc = _bacc.Bacc("TRN2", target_bir_lowering=False, num_devices=1)
    arrays, args = {}, []
    for name in _INS:
        a = _np.ascontiguousarray(inputs[name])
        arrays[f"in_{name}_dram"] = a
        args.append(nc.dram_tensor(f"in_{name}_dram", a.shape, _mybir.dt.from_np(a.dtype), kind="ExternalInput").ap())
    for i, (shape, dtype) in enumerate(_OUTS):
        dt = _mybir.dt.from_np(_np.dtype(dtype))
        args.append(nc.dram_tensor(f"out_{i}_dram", shape, dt, kind="ExternalOutput").ap())
    hybrid_layers(nc, *args)
    r = _run(nc, [arrays], core_ids=[0])
    got = tuple(r.results[0][f"out_{i}_dram"] for i in range(len(_OUTS)))
    return got[0]
```

```python
from contextlib import ExitStack

import concourse.bass as bass
from concourse import mybir

F32 = mybir.dt.float32
F32R = mybir.dt.float32r
ALU = mybir.AluOpType
ACT = mybir.ActivationFunctionType
AX = mybir.AxisListType
ds = bass.ds

C = 128
BANK = 512
QB = 256
QT = QB // C
GROUPS = 32
EPS = 1e-5


def softmax_attention(nc, x, norm_w, norm_b, Wq, bq, Wk, bk, Wv, bv, Wo, bo, t_dram):
    B, _, H, W = x.shape
    N = H * W
    NB = N // QB
    KT = N // C
    STEPS = KT // 2
    KCH = N // BANK
    CH = QT * KCH
    XCH = KCH
    XW = N // XCH
    NCH = 4
    NW = N // NCH
    SCALE = float(C) ** -0.5
    AHEAD = 3
    LAG = 2
    RING = 4
    x_v = x.rearrange("b c h w -> b c (h w)")

    with ExitStack() as ctx:
        def sb(name, shape, dt=F32):
            return ctx.enter_context(nc.sbuf_tensor(name, shape, dt))

        def sem(name):
            return ctx.enter_context(nc.semaphore(name))

        xb = sb("xb", [C, 2, N])
        hn = sb("hn", [C, N])
        k_hi, k_lo = sb("k_hi", [C, N], F32R), sb("k_lo", [C, N], F32R)
        v_hi, v_lo = sb("v_hi", [C, KT, C], F32R), sb("v_lo", [C, KT, C], F32R)
        s_sb = sb("s_sb", [C, 2, QT, N])
        q_hi, q_lo = sb("q_hi", [C, 2, QB], F32R), sb("q_lo", [C, 2, QB], F32R)
        pt_hi, pt_lo = sb("pt_hi", [C, RING, 2, QB], F32R), sb("pt_lo", [C, RING, 2, QB], F32R)
        wq, wk, wv, wo = (sb(n, [C, C]) for n in ("wq", "wk", "wv", "wo"))
        wvo, wvT = sb("wvo", [C, C]), sb("wvT", [C, C])
        ident, gavg = sb("ident", [C, C]), sb("gavg", [C, C])
        cols = sb("cols", [C, 6])
        gnw, gnb, bqc, bkc, bvc, boc = (cols[:, i:i + 1] for i in range(6))
        bvo = sb("bvo", [C, 1])
        bn = sb("bn", [C, KCH, 6])
        mom = sb("mom", [C, 2])
        gst = sb("gst", [C, 8])
        ga, gb = sb("ga", [C, 1]), sb("gb", [C, 1])
        gtmp = sb("gtmp", [C, 1])
        epsc = sb("epsc", [C, 1])
        mx = sb("mx", [C, 2, QT, KCH])
        nmax = sb("nmax", [C, 2, QT])
        rsum = sb("rsum", [C, 2, QT, XCH])
        rden = sb("rden", [C, 2, QT])
        rinv = sb("rinv", [C, 2, QT])
        rb_sb = sb("rb_sb", [C, QB])
        on = sb("on", [C, QB])

        s_ps = ctx.enter_context(nc.psum_tensor("s_ps", [C, 2, BANK], F32))
        pt_ps = ctx.enter_context(nc.psum_tensor("pt_ps", [C, RING, 2, QB], F32))
        om_ps = ctx.enter_context(nc.psum_tensor("om_ps", [C, 2, BANK], F32))

        w_in, x_in, t_out = sem("w_in"), sem("x_in"), sem("t_out")
        const_a, const_b = sem("const_a"), sem("const_b")
        wt_pe, wt_cp, wp_pe, wp_cp = sem("wt_pe"), sem("wt_cp"), sem("wp_pe"), sem("wp_cp")
        bn_done, gn_step, gn_tmp = sem("bn_done"), sem("gn_step"), sem("gn_tmp")
        gn_pe, gn_ln, gn_rs = sem("gn_pe"), sem("gn_ln"), sem("gn_rs")
        h_done = sem("h_done")
        kp_pe, k_h, k_l = sem("kp_pe"), sem("k_h"), sem("k_l")
        vp_pe, v_h, v_l = sem("vp_pe"), sem("v_h"), sem("v_l")
        q_pe, q_h, q_l = sem("q_pe"), sem("q_h"), sem("q_l")
        sc_pe, sc_cp, mx_done = sem("sc_pe"), sem("sc_cp"), sem("mx_done")
        exp_done = sem("exp_done")
        tr_pe, p_hi, p_lo, pv_pe = sem("tr_pe"), sem("p_hi"), sem("p_lo"), sem("pv_pe")
        den_done, inv_done, rb_pe, rb_cp = sem("den_done"), sem("inv_done"), sem("rb_pe"), sem("rb_cp")
        on_done, t_done = sem("on_done"), sem("t_done")

        VG = KT // 4
        BN = KCH + 3
        Q_AT, RB_AT = 5, 11
        X_EARLY = 2
        X_LATE = XCH - X_EARLY
        Q2_AT, RB_LAST = 9, 13

        block = ctx.enter_context(nc.Block())

        def walk(eng, prepare, lead, blk):
            def image(b, more):
                lead(b)
                for p in range(2):
                    blk(b, b * NB + p, p, p)
                with eng.Fori(1, NB // 2 - 1) as j:
                    for p in range(2):
                        blk(b, b * NB + j * 2 + p, j * 2 + p, p, pair=j if more else None)
                for p in range(2):
                    blk(b, b * NB + (NB - 2 + p), NB - 2 + p, p, nxt=b + 1 if more else None)

            prepare()
            with eng.Fori(0, B - 1) as b:
                image(b, True)
            image(B - 1, False)

        def is_at(at, *places):
            return isinstance(at, int) and at in places

        @block.sync
        def _(sp):
            for c in range(2):
                sp.dma_start(xb[:, 0, c * N // 2:(c + 1) * N // 2], x_v[0, :, c * N // 2:(c + 1) * N // 2]).then_inc(x_in, 16)
            for t, d in ((wq, Wq), (wk, Wk), (wv, Wv), (wo, Wo)):
                sp.dma_start(t[:], d).then_inc(w_in, 16)
            for i, d in enumerate((norm_w, norm_b, bq, bk, bv, bo)):
                sp.dma_start(cols[:, i:i + 1], d.rearrange("(c o) -> c o", o=1)).then_inc(w_in, 16)
            for b in range(B):
                if b + 1 < B:
                    sp.wait_ge(x_in, 32 * (b + 1))
                    if b >= 1:
                        sp.wait_ge(t_out, 16 * b * NB // 2)
                    for c in range(2):
                        sp.dma_start(xb[:, (b + 1) % 2, c * N // 2:(c + 1) * N // 2],
                                     x_v[b + 1, :, c * N // 2:(c + 1) * N // 2]).then_inc(x_in, 16)
                with sp.Fori(0, NB // 2) as j:
                    sp.wait_ge(t_done, (j * 2) + (b * NB + 2))
                    sp.dma_start(t_dram[:, ds(j * BANK + b * N, BANK)],
                                 xb[:, b % 2, ds(j * BANK, BANK)]).then_inc(t_out, 16)
            sp.wait_ge(t_out, 16 * B * NB // 2)

        @block.gpsimd
        def _(pool):
            nc.gpsimd.memset(ident[:], 0.0).then_inc(const_a, 1)
            nc.gpsimd.memset(gavg[:], float(GROUPS) / C).then_inc(const_a, 1)
            nc.gpsimd.memset(epsc[:], EPS).then_inc(const_b, 1)
            pool.wait_ge(const_a, 2)
            nc.gpsimd.affine_select(out=ident[:], in_=ident[:], compare_op=ALU.not_equal, fill=1.0, base=0,
                                    pattern=[[-1, C]], channel_multiplier=1).then_inc(const_b, 1)
            per = C // GROUPS
            gv = gavg[:].rearrange("p (g c) -> p g c", c=per)
            nc.gpsimd.affine_select(out=gv, in_=gv, compare_op=ALU.is_ge, fill=0.0, base=0,
                                    pattern=[[-per, GROUPS], [0, per]], channel_multiplier=1).then_inc(const_a, 1)
            pool.wait_ge(const_a, 3)
            nc.gpsimd.affine_select(out=gv, in_=gv, compare_op=ALU.is_ge, fill=0.0, base=per - 1,
                                    pattern=[[per, GROUPS], [0, per]], channel_multiplier=-1).then_inc(const_b, 1)

        @block.tensor
        def _(pe):
            def group_means(b, bank):
                pe.wait_ge(gn_step, b * 4 + 1)
                pe.matmul(om_ps[:, bank, 0:2], gavg[:], mom[:], start=True, stop=True).then_inc(gn_pe, 1)

            def project_q(at, bank):
                pe.matmul(om_ps[:, bank, 0:QB], wq[:], hn[:, ds(at * QB, QB)] if not isinstance(at, int)
                          else hn[:, at * QB:(at + 1) * QB], start=True, stop=True).then_inc(q_pe, 1)

            def project_k(b, g):
                if g % 2 == 0:
                    pe.wait_ge(h_done, b * NCH + (g // 2 + 1))
                if g >= 2:
                    pe.wait_ge(k_l, b * KCH + (g - 1))
                pe.matmul(s_ps[:, g % 2, :], wk[:], hn[:, g * BANK:(g + 1) * BANK],
                          start=True, stop=True).then_inc(kp_pe, 1)

            def project_v(b, g):
                if g >= RING:
                    pe.wait_ge(v_l, b * VG + (g - RING + 1))
                dst = pt_ps[:, g % RING, :, :].rearrange("p k q -> p (k q)")
                for i in range(4):
                    kt = g * 4 + i
                    mm = pe.matmul(dst[:, i * C:(i + 1) * C], hn[:, kt * C:(kt + 1) * C], wvo[:],
                                   start=True, stop=True)
                mm.then_inc(vp_pe, 1)

            def scores(n, par, c, first):
                qt, kc = divmod(c, KCH)
                if c == 0:
                    pe.wait_ge(q_l, n + 1)
                if not (first and c < 2):
                    pe.wait_ge(sc_cp, n * CH + (c - 1))
                qs, ks = slice(qt * C, (qt + 1) * C), slice(kc * BANK, (kc + 1) * BANK)
                dst = s_ps[:, c % 2, :]
                pe.matmul(dst, q_hi[:, par, qs], k_hi[:, ks], start=True, stop=False)
                pe.matmul(dst, q_hi[:, par, qs], k_lo[:, ks], start=False, stop=False)
                pe.matmul(dst, q_lo[:, par, qs], k_hi[:, ks], start=False, stop=True).then_inc(sc_pe, 1)

            def turn(n, par, s, first):
                if s % (STEPS // XCH) == 0:
                    pe.wait_ge(exp_done, n * 2 * XCH + (XCH + s // (STEPS // XCH) + 1))
                if not (first and s < RING):
                    pe.wait_ge(p_lo, n * STEPS + (s - RING + 1))
                for k in range(2):
                    for qt in range(QT):
                        kt = 2 * s + k
                        mm = pe.transpose(pt_ps[:, s % RING, k, qt * C:(qt + 1) * C],
                                          s_sb[:, par, qt, kt * C:(kt + 1) * C], ident[:])
                mm.then_inc(tr_pe, 1)

            def weigh(n, par, s, at):
                pe.wait_ge(p_lo, n * STEPS + (s + 1))
                if s == 0 and not is_at(at, 0):
                    pe.wait_ge(rb_cp, n)
                if s == 0 and not is_at(at, 0, 1):
                    pe.wait_ge(on_done, n - 1)
                o = om_ps[:, par, 0:QB]
                for k in range(2):
                    kt = 2 * s + k
                    pe.matmul(o, v_hi[:, kt, :], pt_hi[:, s % RING, k, :], start=(kt == 0), stop=False)
                    pe.matmul(o, v_lo[:, kt, :], pt_hi[:, s % RING, k, :], start=False, stop=False)
                    mm = pe.matmul(o, v_hi[:, kt, :], pt_lo[:, s % RING, k, :], start=False, stop=(kt == KT - 1))
                mm.then_inc(pv_pe, 1)

            def spread_sums(n, p):
                pe.wait_ge(inv_done, n + 1)
                for qt in range(QT):
                    mm = pe.matmul(om_ps[:, 1 - p, qt * C:(qt + 1) * C],
                                   rinv[:, p, qt:qt + 1].to_broadcast([C, C]), ident[:], start=True, stop=True)
                mm.then_inc(rb_pe, 1)

            def prepare():
                pe.wait_ge(w_in, 160)
                pe.wait_ge(const_b, 3)
                pe.transpose(om_ps[:, 0, 0:C], wv[:], ident[:]).then_inc(wt_pe, 1)
                pe.wait_ge(wt_cp, 1)
                pe.matmul(om_ps[:, 0, 0:C], wvT[:], wo[:], start=True, stop=True)
                pe.matmul(om_ps[:, 0, C:C + 1], wo[:], bvc, start=True, stop=True).then_inc(wp_pe, 1)
                group_means(0, 1)
                pe.wait_ge(wp_cp, 2)
                pe.wait_ge(h_done, 1)
                project_q(0, 0)
                for g in range(KCH):
                    project_k(0, g)
                    if g == 1:
                        pe.wait_ge(q_l, 1)
                        project_q(1, 0)

            def lead(b):
                pe.wait_ge(k_l, b * KCH + KCH)
                for c in range(CH):
                    scores(b * NB, 0, c, True)
                    if c % 2:
                        project_v(b, c // 2)
                pe.wait_ge(v_l, b * VG + VG)

            def blk(b, n, at, p, nxt=None, pair=None):
                first, last = is_at(at, 0), is_at(at, NB - 1)
                ends = is_at(at, NB - 2, NB - 1)
                for c in range(AHEAD):
                    if not last:
                        scores(n + 1, 1 - p, c, False)
                for s in range(STEPS):
                    turn(n, p, s, first)
                    if not last and s + AHEAD < CH:
                        scores(n + 1, 1 - p, s + AHEAD, False)
                    if last and nxt is not None and s % 2 == 0:
                        if s < 4:
                            pe.wait_ge(sc_cp, n * CH + (CH - 1 + s // 2))
                        project_k(nxt, s // 2)
                    if s >= LAG:
                        weigh(n, p, s - LAG, at)
                    elif not first:
                        weigh(n - 1, 1 - p, STEPS - LAG + s, None)
                    if s == Q_AT and not first:
                        pe.wait_ge(on_done, n)
                    if s == Q_AT and not ends:
                        project_q(at + 2, 1 - p)
                    if nxt is not None and is_at(at, NB - 2) and s == Q_AT:
                        group_means(nxt, 1 - p)
                    if nxt is not None and last and s == Q_AT:
                        project_q(0, 1 - p)
                    if nxt is not None and last and s == Q2_AT:
                        pe.wait_ge(q_l, n + 2)
                        project_q(1, 1 - p)
                    if s == (RB_LAST if last else RB_AT):
                        if not ends:
                            pe.wait_ge(q_l, n + 3)
                        elif nxt is not None and last:
                            pe.wait_ge(q_l, n + 3)
                        elif nxt is not None:
                            pe.wait_ge(gn_step, nxt * 4 + 2)
                        spread_sums(n, p)
                if last:
                    for s in range(STEPS - LAG, STEPS):
                        weigh(n, p, s, at)

            walk(pe, prepare, lead, blk)

        @block.scalar
        def _(act):
            def split_q(n, par, bank):
                act.wait_ge(q_pe, n + 1)
                nc.scalar.activation(q_hi[:, par, :], om_ps[:, bank, 0:QB], ACT.Identity, bias=bqc).then_inc(q_h, 1)

            def split_k(b, g):
                act.wait_ge(kp_pe, b * KCH + (g + 1))
                nc.scalar.activation(k_hi[:, g * BANK:(g + 1) * BANK], s_ps[:, g % 2, :], ACT.Identity,
                                     bias=bkc).then_inc(k_h, 1)

            def exps(n, par, qt, c):
                if c == 0:
                    act.wait_ge(mx_done, n * QT + (qt + 1))
                sl = s_sb[:, par, qt, c * XW:(c + 1) * XW]
                nc.scalar.activation(sl, sl, ACT.Exp, bias=nmax[:, par, qt:qt + 1],
                                     accum_out=rsum[:, par, qt, c:c + 1]).then_inc(exp_done, 1)

            def group_scale(b):
                act.wait_ge(gn_step, b * 4 + 3)
                nc.scalar.activation(gst[:, 4:5], gst[:, 3:4], ACT.Ln, bias=epsc[:]).then_inc(gn_ln, 1)
                act.wait_ge(gn_ln, b + 1)
                nc.scalar.activation(gst[:, 5:6], gst[:, 4:5], ACT.Exp, scale=-0.5).then_inc(gn_rs, 1)

            def normalise(b, c):
                if c == 0:
                    act.wait_ge(gn_step, b * 4 + 4)
                xs = xb[:, b % 2 if isinstance(b, int) else ds(b % 2, 1), c * NW:(c + 1) * NW]
                nc.scalar.activation(hn[:, c * NW:(c + 1) * NW], xs, ACT.Identity, bias=gb[:],
                                     scale=ga[:]).then_inc(h_done, 1)

            def prepare():
                nc.scalar.preload_act_table_set("natural_log_exp_and_others")
                act.wait_ge(wt_pe, 1)
                nc.scalar.copy(wvT[:], om_ps[:, 0, 0:C]).then_inc(wt_cp, 1)
                act.wait_ge(wp_pe, 1)
                nc.scalar.copy(wvo[:], om_ps[:, 0, 0:C]).then_inc(wp_cp, 1)
                group_scale(0)
                for c in range(NCH):
                    normalise(0, c)
                    if c == 0:
                        split_q(0, 0, 0)
                for g in range(KCH):
                    split_k(0, g)
                    if g == 1:
                        split_q(1, 1, 0)

            def lead(b):
                for g in range(VG):
                    act.wait_ge(vp_pe, b * VG + (g + 1))
                    nc.scalar.copy(v_hi[:, g * 4:g * 4 + 4, :].rearrange("p a c -> p (a c)"),
                                   pt_ps[:, g % RING, :, :].rearrange("p k q -> p (k q)")).then_inc(v_h, 1)
                    if g >= VG // 2:
                        for c in range(2):
                            exps(b * NB, 0, 0, (g - VG // 2) * 2 + c)
                for c in range(X_EARLY):
                    exps(b * NB, 0, 1, c)

            def blk(b, n, at, p, nxt=None, pair=None):
                first, last = is_at(at, 0), is_at(at, NB - 1)
                ends = is_at(at, NB - 2, NB - 1)
                for s in range(STEPS):
                    act.wait_ge(tr_pe, n * STEPS + (s + 1))
                    if not (first and s < RING):
                        act.wait_ge(pv_pe, n * STEPS + (s - RING + 1))
                    nc.scalar.copy(pt_hi[:, s % RING, :, :], pt_ps[:, s % RING, :, :]).then_inc(p_hi, 1)
                    if s < X_LATE:
                        exps(n, p, 1, X_EARLY + s)
                    elif not last:
                        exps(n + 1, 1 - p, (s - X_LATE) // XCH, (s - X_LATE) % XCH)
                    if nxt is not None and is_at(at, NB - 2):
                        if s == Q_AT + 1:
                            group_scale(nxt)
                        if s in (9, 11, 13, 15):
                            normalise(nxt, (s - 9) // 2)
                    if nxt is not None and last:
                        if s % 2:
                            split_k(nxt, s // 2)
                        if s == Q_AT + 1:
                            split_q(n + 1, 0, 1 - p)
                        if s == Q2_AT + 1:
                            split_q(n + 2, 1, 1 - p)
                    if s == Q_AT and not ends:
                        split_q(n + 2, p, 1 - p)
                    if s == (RB_LAST if last else RB_AT):
                        act.wait_ge(rb_pe, n + 1)
                        if not first:
                            act.wait_ge(on_done, n)
                        nc.scalar.copy(rb_sb[:], om_ps[:, 1 - p, 0:QB]).then_inc(rb_cp, 1)

            walk(act, prepare, lead, blk)

        @block.vector
        def _(dve):
            def split_q(n, par, bank):
                dve.wait_ge(q_h, n + 1)
                nc.vector.scalar_tensor_tensor(out=q_lo[:, par, :], in0=om_ps[:, bank, 0:QB], scalar=bqc,
                                               in1=q_hi[:, par, :].bitcast(F32), op0=ALU.add,
                                               op1=ALU.subtract).then_inc(q_l, 1)

            def split_k(b, g):
                dve.wait_ge(k_h, b * KCH + (g + 1))
                sl = slice(g * BANK, (g + 1) * BANK)
                nc.vector.scalar_tensor_tensor(out=k_lo[:, sl], in0=s_ps[:, g % 2, :], scalar=bkc,
                                               in1=k_hi[:, sl].bitcast(F32), op0=ALU.add,
                                               op1=ALU.subtract).then_inc(k_l, 1)

            def score_copy(n, par, c):
                qt, kc = divmod(c, KCH)
                dve.wait_ge(sc_pe, n * CH + (c + 1))
                nc.vector.tensor_scalar(s_sb[:, par, qt, kc * BANK:(kc + 1) * BANK], s_ps[:, c % 2, :],
                                        SCALE, None, ALU.mult, ALU.max,
                                        accum_out=mx[:, par, qt, kc:kc + 1]).then_inc(sc_cp, 1)
                if kc == KCH - 1:
                    dve.wait_ge(sc_cp, n * CH + (c + 1))
                    nc.vector.tensor_reduce(nmax[:, par, qt:qt + 1], mx[:, par, qt, :], AX.X, ALU.max,
                                            negate=True).then_inc(mx_done, 1)

            def finish(n, at, par, bpar):
                dve.wait_ge(pv_pe, n * STEPS + STEPS)
                dve.wait_ge(rb_cp, n + 1)
                nc.vector.tensor_tensor(on[:], om_ps[:, par, 0:QB], rb_sb[:], ALU.mult).then_inc(on_done, 1)
                dve.wait_ge(on_done, n + 1)
                xs = xb[:, ds(bpar, 1), ds(at * QB, QB)].rearrange("c o n -> c (o n)")
                nc.vector.scalar_tensor_tensor(out=xs, in0=on[:], scalar=bvo[:], in1=xs, op0=ALU.add,
                                               op1=ALU.add).then_inc(t_done, 1)

            def moments(b, c):
                xs = xb[:, b % 2 if isinstance(b, int) else ds(b % 2, 1),
                        c * BANK:(c + 1) * BANK] if isinstance(c, int) else xb[:, ds(b % 2, 1), ds(c * BANK, BANK)]
                dst = bn[:, c, :] if isinstance(c, int) else bn[:, ds(c, 1), :]
                nc.vector.bn_stats(dst, xs).then_inc(bn_done, 1)

            def channel_moments(b):
                dve.wait_ge(bn_done, b * BN + KCH)
                nc.vector.memset(gst[:, 6:7], 0.0)
                nc.vector.bn_aggr(mom[:], bn[:].rearrange("p a s -> p (a s)")).then_inc(bn_done, 1)
                dve.wait_ge(bn_done, b * BN + (KCH + 1))
                nc.vector.tensor_tensor(gtmp[:], mom[:, 0:1], mom[:, 0:1], ALU.mult).then_inc(bn_done, 1)
                dve.wait_ge(bn_done, b * BN + (KCH + 2))
                nc.vector.tensor_tensor(mom[:, 1:2], mom[:, 1:2], gtmp[:], ALU.add).then_inc(gn_step, 1)

            def group_variance(b, bank):
                dve.wait_ge(gn_pe, b + 1)
                nc.vector.tensor_copy(gst[:, 0:2], om_ps[:, bank, 0:2]).then_inc(gn_step, 1)
                dve.wait_ge(gn_step, b * 4 + 2)
                nc.vector.scalar_tensor_tensor(out=gst[:, 2:3], in0=gst[:, 0:1], scalar=gst[:, 0:1],
                                               in1=gst[:, 1:2], op0=ALU.mult, op1=ALU.subtract).then_inc(gn_tmp, 1)
                dve.wait_ge(gn_tmp, b * 2 + 1)
                nc.vector.tensor_scalar(gst[:, 3:4], gst[:, 2:3], -1.0, 0.0, ALU.mult, ALU.max).then_inc(gn_step, 1)

            def scale_shift(b):
                dve.wait_ge(gn_rs, b + 1)
                nc.vector.tensor_tensor(ga[:], gst[:, 5:6], gnw, ALU.mult).then_inc(gn_tmp, 1)
                dve.wait_ge(gn_tmp, b * 2 + 2)
                nc.vector.tensor_tensor(gtmp[:], gst[:, 0:1], ga[:], ALU.mult).then_inc(bn_done, 1)
                dve.wait_ge(bn_done, b * BN + BN)
                nc.vector.tensor_tensor(gb[:], gnb, gtmp[:], ALU.subtract).then_inc(gn_step, 1)

            def prepare():
                dve.wait_ge(x_in, 32)
                for c in range(KCH):
                    moments(0, c)
                channel_moments(0)
                dve.wait_ge(wp_pe, 1)
                dve.wait_ge(wp_cp, 1)
                nc.vector.tensor_tensor(bvo[:], om_ps[:, 0, C:C + 1], boc, ALU.add).then_inc(wp_cp, 1)
                group_variance(0, 1)
                scale_shift(0)
                split_q(0, 0, 0)
                for g in range(KCH):
                    split_k(0, g)
                    if g == 1:
                        split_q(1, 1, 0)

            def lead(b):
                for c in range(CH):
                    score_copy(b * NB, 0, c)
                    if c % 2:
                        g = c // 2
                        dve.wait_ge(v_h, b * VG + (g + 1))
                        dst = slice(g * 4, g * 4 + 4)
                        nc.vector.tensor_tensor(v_lo[:, dst, :].rearrange("p a c -> p (a c)"),
                                                pt_ps[:, g % RING, :, :].rearrange("p k q -> p (k q)"),
                                                v_hi[:, dst, :].rearrange("p a c -> p (a c)").bitcast(F32),
                                                ALU.subtract).then_inc(v_l, 1)

            def blk(b, n, at, p, nxt=None, pair=None):
                first, last = is_at(at, 0), is_at(at, NB - 1)
                ends = is_at(at, NB - 2, NB - 1)
                if not last:
                    for c in range(AHEAD - 1):
                        score_copy(n + 1, 1 - p, c)
                for s in range(STEPS):
                    if pair is not None and p == 0 and s == 1 or nxt is not None and is_at(at, NB - 2) and s == 0:
                        dve.wait_ge(x_in, b * 32 + 64)
                    if not last and s + AHEAD - 1 < CH:
                        score_copy(n + 1, 1 - p, s + AHEAD - 1)
                    dve.wait_ge(p_hi, n * STEPS + (s + 1))
                    nc.vector.tensor_tensor(pt_lo[:, s % RING, :, :], pt_ps[:, s % RING, :, :],
                                            pt_hi[:, s % RING, :, :].bitcast(F32), ALU.subtract).then_inc(p_lo, 1)
                    if s == LAG + 1 and not first:
                        finish(n - 1, at - 1, 1 - p, b % 2)
                    if pair is not None and p == 0 and s == 1:
                        moments(b + 1, pair - 1)
                    if nxt is not None and is_at(at, NB - 2):
                        if s < 2:
                            moments(nxt, KCH - 2 + s)
                        if s == 2:
                            channel_moments(nxt)
                        if s == Q_AT + 1:
                            group_variance(nxt, 1 - p)
                        if s == Q_AT + 2:
                            scale_shift(nxt)
                    if nxt is not None and last:
                        if s % 2:
                            split_k(nxt, s // 2)
                        if s == Q_AT + 2:
                            split_q(n + 1, 0, 1 - p)
                        if s == Q2_AT + 2:
                            split_q(n + 2, 1, 1 - p)
                    if s == Q_AT + 1 and not ends:
                        split_q(n + 2, p, 1 - p)
                    if s == 9:
                        dve.wait_ge(exp_done, n * 2 * XCH + 2 * XCH)
                        nc.vector.tensor_reduce(rden[:, p, :], rsum[:, p, :, :], AX.X, ALU.add).then_inc(den_done, 1)
                        dve.wait_ge(den_done, n + 1)
                        nc.vector.reciprocal(rinv[:, p, :], rden[:, p, :]).then_inc(inv_done, 1)
                if last:
                    finish(n, at, p, b % 2)

            walk(dve, prepare, lead, blk)


def scan_attention_and_experts(nc, t_dram, W_kv, q_proj, router_w, router_b, expert_w, expert_b, out):
    B, _, H, W = out.shape
    N = H * W
    HEADS = q_proj.shape[0]
    E = router_w.shape[1]
    TOK = BANK
    PER = N // TOK
    NBLK = B * PER
    TT = TOK // C
    QUAD, HALF = 32, 16
    LOWEST = -3.0e38
    out_v = out.rearrange("b c h w -> b c (h w)")

    with ExitStack() as ctx:
        def sb(name, shape, dt=F32):
            return ctx.enter_context(nc.sbuf_tensor(name, shape, dt))

        def psum(name, shape):
            return ctx.enter_context(nc.psum_tensor(name, shape, F32))

        def sem(name):
            return ctx.enter_context(nc.semaphore(name))

        t = sb("t", [C, NBLK * TOK])
        wkv = sb("wkv", [C, HEADS, 2, C])
        w_hi, w_lo = sb("w_hi", [C, HEADS, 2, C], F32R), sb("w_lo", [C, HEADS, 2, C], F32R)
        qcol = sb("qcol", [C, HEADS])
        qz = sb("qz", [C, HEADS, QUAD])
        rw = sb("rw", [C, E])
        rbias = sb("rbias", [C, E])
        ew = sb("ew", [C, E, C])
        eb = sb("eb", [C, C])
        eb_hi, eb_lo = sb("eb_hi", [C, C], F32R), sb("eb_lo", [C, C], F32R)
        ident, center, mean_w = sb("ident1", [C, C]), sb("center", [C, C]), sb("mean_w", [C, C])
        sel_h = sb("sel_h", [C, HEADS, C], F32R)
        sel_e = sb("sel_e", [C, E, C], F32R)
        low_rows4, low_rows = sb("low_rows4", [C, 4]), sb("low_rows", [C, 1])
        before = sb("before", [C, E, E])
        place_i = sb("place_i", [C, E])
        zeros = sb("zeros", [C, TOK])
        epsc = sb("epsc1", [C, 1])

        ln_sq, ln_l, ln_r = sb("ln_sq", [C, TOK]), sb("ln_l", [C, TOK]), sb("ln_r", [C, TOK])
        xf = sb("xf", [C, TOK])
        xn_hi, xn_lo = sb("xn_hi", [C, 2, TOK], F32R), sb("xn_lo", [C, 2, TOK], F32R)
        xn2 = sb("xn2", [C, 2, TOK])
        sk = sb("sk", [C, HEADS, TOK])
        sv = sb("sv", [C, 3, TOK])
        m_r, d_r, e_r, u_r = (sb(n, [C, TOK]) for n in ("m_r", "d_r", "e_r", "u_r"))
        l_r, b_r, a_r = (sb(n, [C, TOK]) for n in ("l_r", "b_r", "a_r"))
        zr = sb("zr", [C, 2, TOK], F32R)
        new_w, old_w = sb("new_w", [C, TOK], F32R), sb("old_w", [C, TOK], F32R)
        z = sb("z", [C, 2, TOK])
        y = sb("y", [C, HEADS, TOK])
        acc = sb("acc", [C, TOK])
        xg = sb("xg", [C, 3, TOK])
        lg = sb("lg", [C, TT, E])
        ge, gel = sb("ge", [C, TT, E, E]), sb("gel", [C, TT, E, E])
        r1, r2, rank, pick = (sb(n, [C, TT, E]) for n in ("r1", "r2", "rank", "pick"))
        sl, dl, th, g1, g2 = (sb(n, [C, TT, E]) for n in ("sl", "dl", "th", "g1", "g2"))
        ssum = sb("ssum", [C, TT])
        ghr = sb("ghr", [C, TT, E], F32R)
        g16 = sb("g16", [C, TT, 2 * E])
        gt = sb("gt", [C, TOK], F32R)

        kv_ps = psum("kv_ps", [C, 2, BANK])
        bc_ps = psum("bc_ps", [C, 2, BANK])
        row_ps = psum("row_ps", [C, BANK])
        mo_ps = psum("mo_ps", [C, BANK])
        lnd_ps = psum("lnd_ps", [C, BANK])
        lnv_ps = psum("lnv_ps", [C, BANK])

        names = """w_in t_in t_out cst1 cst2 cst3 wt_pe wt_hi wt_lo
            k_pe s_pe v_pe bc_pe g_pe x_pe c1_pe w1_pe c2_pe w2_pe r_pe gt_pe
            k_act v_act sq1 sq2 ln1 ln2 rs1 rs2 hi_act e_act lu_act b_act th_act gt_act
            z_dve y_dve m_dve d_dve u_dve l_dve rows_dve xf_dve lo_dve xn2_dve xg_dve t2_dve out_dve gate g16_dve
            acc_pool""".split()
        (w_in, t_in, t_out, cst1, cst2, cst3, wt_pe, wt_hi, wt_lo,
         k_pe, s_pe, v_pe, bc_pe, g_pe, x_pe, c1_pe, w1_pe, c2_pe, w2_pe, r_pe, gt_pe,
         k_act, v_act, sq1, sq2, ln1, ln2, rs1, rs2, hi_act, e_act, lu_act, b_act, th_act, gt_act,
         z_dve, y_dve, m_dve, d_dve, u_dve, l_dve, rows_dve, xf_dve, lo_dve, xn2_dve, xg_dve, t2_dve, out_dve,
         gate, g16_dve, acc_pool) = (sem(n) for n in names)
        GATE = 12
        ROWS = 5

        block = ctx.enter_context(nc.Block())

        def at_least(eng, s, value):
            if not (isinstance(value, int) and value <= 0):
                eng.wait_ge(s, value)

        def walk(eng, it):
            def pair(n, first, last=False):
                for p in range(2):
                    it(n + p, p, keys=True, values=not (isinstance(n, int) and n + p < 1),
                       experts=not (isinstance(n, int) and n + p < 2), norm=not (last and p == 1),
                       new_rows=first and p == 0, new_values=first and p == 1)

            pair(0, True)
            with eng.Fori(1, PER // 2) as j:
                pair(j * 2, False)
            with eng.Fori(1, B - 1) as b:
                pair(b * PER, True)
                with eng.Fori(1, PER // 2) as j:
                    pair(b * PER + j * 2, False)
            pair((B - 1) * PER, True)
            with eng.Fori(1, PER // 2 - 1) as j:
                pair(j * 2 + (B - 1) * PER, False)
            pair(NBLK - 2, False, True)
            it(NBLK, 0, keys=False, values=True, experts=True, norm=False, new_rows=False, new_values=False)
            it(NBLK + 1, 1, keys=False, values=False, experts=True, norm=False, new_rows=False, new_values=False)

        def tok(n):
            return slice(n * TOK, (n + 1) * TOK) if isinstance(n, int) else ds(n * TOK, TOK)

        @block.sync
        def _(sp):
            sp.dma_start(wkv[:], W_kv.rearrange("(h d two) c -> d h two c", h=HEADS, two=2)).then_inc(w_in, 16)
            sp.dma_start(qcol[:], q_proj.rearrange("h d -> d h"), allow_slow_non_contiguous=True).then_inc(w_in, 16)
            sp.dma_start(rw[:], router_w).then_inc(w_in, 16)
            sp.dma_start(rbias[:], router_b.rearrange("(o e) -> o e", o=1).to_broadcast([C, E])).then_inc(w_in, 16)
            sp.dma_start(ew[:], expert_w.rearrange("e c d -> c e d")).then_inc(w_in, 16)
            sp.wait_ge(cst2, 1)
            for i in range(2):
                sp.dma_start(eb[i * E:(i + 1) * E, :], expert_b).then_inc(w_in, 16)
            for b in range(B):
                if b:
                    sp.wait_ge(t_in, 16 * b)
                sp.dma_start(t[:, b * N:(b + 1) * N], t_dram[:, b * N:(b + 1) * N]).then_inc(t_in, 16)
            for b in range(B):
                with sp.Fori(0, PER) as j:
                    sp.wait_ge(out_dve, j + (b * PER + 1))
                    sp.dma_start(out_v[b, :, ds(j * TOK, TOK)], t[:, ds(j * TOK + b * N, TOK)]).then_inc(t_out, 16)
            sp.wait_ge(t_out, 16 * NBLK)

        @block.gpsimd
        def _(pool):
            nc.gpsimd.memset(eb[:], 0.0).then_inc(cst2, 1)
            nc.gpsimd.memset(ident[:], 0.0).then_inc(cst1, 1)
            nc.gpsimd.memset(low_rows4[:], 1.0).then_inc(cst1, 1)
            nc.gpsimd.memset(before[:], 1.0).then_inc(cst1, 1)
            nc.gpsimd.memset(mean_w[:], 1.0 / C).then_inc(cst1, 1)
            nc.gpsimd.memset(epsc[:], EPS).then_inc(cst1, 1)
            nc.gpsimd.memset(zeros[:], 0.0).then_inc(cst1, 1)
            nc.gpsimd.memset(qz[:], 0.0).then_inc(cst1, 1)
            nc.gpsimd.memset(gt[:].bitcast(F32), 0.0).then_inc(cst1, 1)
            pool.wait_ge(cst1, 8)
            nc.gpsimd.affine_select(out=ident[:], in_=ident[:], compare_op=ALU.not_equal, fill=1.0, base=0,
                                    pattern=[[-1, C]], channel_multiplier=1).then_inc(cst3, 1)
            nc.gpsimd.affine_select(out=before[:], in_=before[:], compare_op=ALU.is_gt, fill=0.0, base=0,
                                    pattern=[[1, E], [-1, E]], channel_multiplier=0).then_inc(cst3, 1)
            nc.gpsimd.affine_select(out=low_rows4[:], in_=low_rows4[:], compare_op=ALU.is_ge, fill=0.0, base=-HALF,
                                    pattern=[[-QUAD, 4]], channel_multiplier=1).then_inc(cst1, 1)
            pool.wait_ge(cst1, 9)
            nc.gpsimd.affine_select(out=low_rows4[:], in_=low_rows4[:], compare_op=ALU.is_ge, fill=0.0,
                                    base=QUAD - 1, pattern=[[QUAD, 4]], channel_multiplier=-1).then_inc(cst3, 1)

            def it(n, p, keys, values, experts, norm, new_rows, new_values):
                if not values:
                    return
                v = n - 1
                at_least(pool, t2_dve, v)
                for h in range(1, HEADS):
                    pool.wait_ge(y_dve, v * HEADS + (h + 1))
                    if h > 1:
                        pool.wait_ge(acc_pool, v * (HEADS - 1) + (h - 1))
                    nc.gpsimd.tensor_tensor(acc[:], y[:, 0, :] if h == 1 else acc[:], y[:, h, :],
                                            ALU.add).then_inc(acc_pool, 1)

            walk(pool, it)

        @block.tensor
        def _(pe):
            pe.wait_ge(w_in, 16 * 7)
            pe.wait_ge(cst3, 5)
            for g in range(2 * HEADS // TT):
                if g >= 2:
                    pe.wait_ge(wt_lo, g - 1)
                for i in range(TT):
                    h, two = divmod(g * TT + i, 2)
                    mm = pe.transpose(kv_ps[:, g % 2, i * C:(i + 1) * C], wkv[:, h, two, :], ident[:])
                mm.then_inc(wt_pe, 1)
            pe.wait_ge(wt_lo, 2 * HEADS // TT)

            def project(dst, head, two, par):
                pe.matmul(dst, w_hi[:, head, two, :], xn_hi[:, par, :], start=True, stop=False)
                pe.matmul(dst, w_hi[:, head, two, :], xn_lo[:, par, :], start=False, stop=False)
                return pe.matmul(dst, w_lo[:, head, two, :], xn_hi[:, par, :], start=False, stop=True)

            def row_sums(n, j):
                if j == 0:
                    at_least(pe, d_dve, n)
                pe.wait_ge(k_act, n * HEADS + (4 * j + 4))
                for g in range(4):
                    h = 4 * j + g
                    mm = pe.matmul(row_ps[QUAD * g:QUAD * (g + 1), :], qz[:, h, :], sk[:, h, :],
                                   start=(j == 0), stop=(j == 1))
                if j == 1:
                    mm.then_inc(s_pe, 1)

            def norm_center(n, s_in, free, s_out):
                if s_in is not None:
                    pe.wait_ge(s_in, n + 1)
                at_least(pe, *free)
                pe.matmul(lnd_ps[:], center[:], t[:, tok(n)], start=True, stop=True).then_inc(s_out, 1)

            def norm_var(n, sq, free, s_out):
                pe.wait_ge(sq, n + 1)
                at_least(pe, *free)
                pe.matmul(lnv_ps[:], mean_w[:], ln_sq[:], start=True, stop=True).then_inc(s_out, 1)

            pe.wait_ge(t_in, 16)
            norm_center(0, None, (xn2_dve, 0), c1_pe)
            norm_var(0, sq1, (gt_act, 0), w1_pe)

            def it(n, p, keys, values, experts, norm, new_rows, new_values):
                v, q = n - 1, n - 2
                if keys:
                    pe.wait_ge(lo_dve, n + 1)
                    for h in range(HEADS):
                        if h == 0:
                            at_least(pe, v_act, (n - 1) * HEADS)
                        if h >= 2:
                            pe.wait_ge(k_act, n * HEADS + (h - 1))
                        project(kv_ps[:, h % 2, :], h, 0, p).then_inc(k_pe, 1)
                        if h == 1 and experts:
                            router(q, p)
                        if h == 5:
                            row_sums(n, 0)
                elif experts:
                    router(q, p)
                if values:
                    for h in range(HEADS):
                        if h < 2 and keys:
                            pe.wait_ge(k_act, n * HEADS + (HEADS - 1 + h))
                        elif h < 2:
                            pe.wait_ge(v_act, v * HEADS)
                        else:
                            pe.wait_ge(v_act, v * HEADS + (h - 1))
                        project(kv_ps[:, h % 2, :], h, 1, 1 - p).then_inc(v_pe, 1)
                        if h == 0:
                            pe.wait_ge(rows_dve, v * ROWS + ROWS)
                        else:
                            pe.wait_ge(z_dve, v * HEADS + h)
                        pe.matmul(bc_ps[:, 0, :], sel_h[:, h, :], new_w[:], start=True, stop=True)
                        if h:
                            pe.wait_ge(y_dve, v * HEADS + h)
                        pe.matmul(bc_ps[:, 1, :], sel_h[:, h, :], old_w[:], start=True, stop=True).then_inc(bc_pe, 1)
                        if h == 1 and keys:
                            row_sums(n, 1)
                        if h == 3 and experts:
                            turn_gates(q)
                elif keys:
                    row_sums(n, 1)
                if not values and experts:
                    turn_gates(q)
                if experts:
                    pe.wait_ge(gt_act, q + 1)
                    if not values:
                        pe.wait_ge(out_dve, q)
                    pe.matmul(mo_ps[:], eb_hi[:], gt[:], start=True, stop=False)
                    pe.matmul(mo_ps[:], eb_lo[:], gt[:], start=False, stop=False)
                    if values:
                        pe.wait_ge(y_dve, v * HEADS + HEADS)
                    spread(q, 0)
                    spread(q, 1)
                for e in range(E):
                    if experts:
                        pe.wait_ge(xg_dve, q * E + (e + 1))
                        if e + 2 < E:
                            spread(q, e + 2)
                        pe.matmul(mo_ps[:], ew[:, e, :], xg[:, e % 3, :], start=False,
                                  stop=(e == E - 1)).then_inc(x_pe, 1)
                    if norm and e == 0:
                        if n_is(n, 0) or not isinstance(n, int) or n % PER == PER - 1:
                            pe.wait_ge(t_in, norm_image(n))
                        norm_center(n + 1, None, (xn2_dve, n - 1), c1_pe)
                    if norm and e == 2:
                        norm_var(n + 1, sq1, (gt_act, n - 1), w1_pe)
                    if values and e == 4:
                        if norm:
                            norm_center(v, t2_dve, (xf_dve, n + 2), c2_pe)
                        else:
                            norm_center(v, t2_dve, (xn2_dve, v), c2_pe)
                    if values and e == 6:
                        norm_var(v, sq2, (ln1, n + 2 if norm else NBLK), w2_pe)

            def n_is(n, k):
                return isinstance(n, int) and n == k

            def norm_image(n):
                return 16 * (1 if isinstance(n, int) and n + 1 < PER else B)

            def spread(q, e):
                if e >= 2:
                    pass
                pe.matmul(bc_ps[:, e % 2, :], sel_e[:, e, :], gt[:], start=True, stop=True).then_inc(g_pe, 1)

            def router(q, p):
                pe.wait_ge(xn2_dve, q + 1)
                for i in range(TT):
                    mm = pe.matmul(lnv_ps[:, i * E:(i + 1) * E], xn2[:, p, i * C:(i + 1) * C], rw[:],
                                   start=True, stop=True)
                mm.then_inc(r_pe, 1)

            def turn_gates(q):
                pe.wait_ge(g16_dve, 2 * q + 2)
                for i in range(TT):
                    mm = pe.transpose(lnv_ps[0:2 * E, i * C:(i + 1) * C], g16[:, i, :], ident[:])
                mm.then_inc(gt_pe, 1)

            walk(pe, it)

        @block.scalar
        def _(act):
            for g in range(2 * HEADS // TT):
                act.wait_ge(wt_pe, g + 1)
                dst = w_hi[:].rearrange("p h w c -> p (h w c)")[:, g * BANK:(g + 1) * BANK]
                nc.scalar.copy(dst, kv_ps[:, g % 2, :]).then_inc(wt_hi, 1)

            def norm_pre(n, c_pe, free, sq):
                act.wait_ge(c_pe, n + 1)
                at_least(act, *free)
                nc.scalar.activation(ln_sq[:], lnd_ps[:], ACT.Square).then_inc(sq, 1)

            def norm_post(n, w_pe, free, ln, rs):
                act.wait_ge(w_pe, n + 1)
                nc.scalar.activation(ln_l[:], lnv_ps[:], ACT.Ln, bias=epsc[:]).then_inc(ln, 1)
                act.wait_ge(ln, n + 1)
                at_least(act, *free)
                nc.scalar.activation(ln_r[:], ln_l[:], ACT.Exp, scale=-0.5).then_inc(rs, 1)

            def high(n, par):
                act.wait_ge(xf_dve, n + 1)
                at_least(act, v_pe, (n - 1) * HEADS)
                nc.scalar.copy(xn_hi[:, par, :], xf[:]).then_inc(hi_act, 1)

            nc.scalar.preload_act_table_set("natural_log_exp_and_others")
            act.wait_ge(cst3, 3)
            norm_pre(0, c1_pe, (w2_pe, 0), sq1)
            norm_post(0, w1_pe, (xn2_dve, 0), ln1, rs1)
            high(0, 0)

            def it(n, p, keys, values, experts, norm, new_rows, new_values):
                v, q = n - 1, n - 2

                def gates():
                    act.wait_ge(gate, q * GATE + 9)
                    nc.scalar.activation(th[:], dl[:], ACT.Tanh).then_inc(th_act, 1)

                if keys or values:
                    nc.scalar.preload_act_table_set("silu_and_others")
                if keys:
                    at_least(act, s_pe, n)
                    for h in range(HEADS):
                        act.wait_ge(k_pe, n * HEADS + (h + 1))
                        nc.scalar.activation(sk[:, h, :], kv_ps[:, h % 2, :], ACT.Silu).then_inc(k_act, 1)
                if experts:
                    gates()
                if values:
                    for h in range(HEADS):
                        act.wait_ge(v_pe, v * HEADS + (h + 1))
                        at_least(act, z_dve, v * HEADS + (h - 2))
                        nc.scalar.activation(sv[:, h % 3, :], kv_ps[:, h % 2, :], ACT.Silu).then_inc(v_act, 1)
                        if h == 4 and experts:
                            turned(q)
                elif experts:
                    turned(q)
                nc.scalar.preload_act_table_set("natural_log_exp_and_others")
                if norm:
                    norm_pre(n + 1, c1_pe, (w2_pe, n - 1), sq1)
                if keys:
                    act.wait_ge(d_dve, n + 1)
                    nc.scalar.activation(e_r[:], d_r[:], ACT.Exp).then_inc(e_act, 1)
                if norm:
                    norm_post(n + 1, w1_pe, (xn2_dve, n - 1), ln1, rs1)
                if keys:
                    act.wait_ge(u_dve, n + 1)
                    nc.scalar.activation(l_r[:], u_r[:], ACT.Ln).then_inc(lu_act, 1)
                if norm:
                    high(n + 1, 1 - p)
                if keys:
                    act.wait_ge(l_dve, n + 1)
                    nc.scalar.activation(b_r[:], e_r[:], ACT.Exp).then_inc(b_act, 1)
                if values:
                    norm_pre(v, c2_pe, (w1_pe, n + 2 if norm else NBLK), sq2)
                    norm_post(v, w2_pe, (xf_dve, n + 2 if norm else NBLK), ln2, rs2)

            def turned(q):
                act.wait_ge(gt_pe, q + 1)
                nc.scalar.copy(gt[0:2 * E, :], lnv_ps[0:2 * E, :]).then_inc(gt_act, 1)

            walk(act, it)

        @block.vector
        def _(dve):
            dve.wait_ge(cst3, 3)
            dve.wait_ge(w_in, 16 * 7)
            nc.vector.tensor_scalar(center[:], ident[:], -1.0 / C, None, ALU.add).then_inc(cst3, 1)
            for h in range(HEADS):
                r0 = QUAD * (h % 4) + h // 4
                nc.vector.tensor_tensor(sel_h[:, h, :], ident[:, r0:r0 + 1].to_broadcast([C, C]),
                                        ident[:, r0 + HALF:r0 + HALF + 1].to_broadcast([C, C]), ALU.add)
                for col in (h // 4, h // 4 + HALF):
                    nc.vector.tensor_copy(qz[:, h, col:col + 1], qcol[:, h:h + 1])
            for e in range(E):
                nc.vector.tensor_tensor(sel_e[:, e, :], ident[:, e:e + 1].to_broadcast([C, C]),
                                        ident[:, e + E:e + E + 1].to_broadcast([C, C]), ALU.add)
            nc.vector.tensor_reduce(low_rows[:], low_rows4[:], AX.X, ALU.add).then_inc(cst2, 1)
            nc.vector.tensor_reduce(place_i[:], before[:], AX.X, ALU.add).then_inc(cst2, 1)
            nc.vector.tensor_copy(eb_hi[:], eb[:]).then_inc(cst2, 1)
            dve.wait_ge(cst2, 4)
            nc.vector.tensor_scalar(place_i[:], place_i[:], -5.0, None, ALU.add).then_inc(cst2, 1)
            nc.vector.tensor_tensor(eb_lo[:], eb[:], eb_hi[:].bitcast(F32), ALU.subtract).then_inc(cst3, 1)
            for g in range(2 * HEADS // TT):
                dve.wait_ge(wt_hi, g + 1)
                sl_ = slice(g * BANK, (g + 1) * BANK)
                nc.vector.tensor_tensor(w_lo[:].rearrange("p h w c -> p (h w c)")[:, sl_], kv_ps[:, g % 2, :],
                                        w_hi[:].rearrange("p h w c -> p (h w c)")[:, sl_].bitcast(F32),
                                        ALU.subtract).then_inc(wt_lo, 1)

            def norm_one(n, par):
                dve.wait_ge(rs1, n + 1)
                at_least(dve, hi_act, n)
                at_least(dve, lo_dve, n)
                nc.vector.tensor_tensor(xf[:], lnd_ps[:], ln_r[:], ALU.mult).then_inc(xf_dve, 1)

            def low(n, par):
                dve.wait_ge(hi_act, n + 1)
                nc.vector.tensor_tensor(xn_lo[:, par, :], xf[:], xn_hi[:, par, :].bitcast(F32),
                                        ALU.subtract).then_inc(lo_dve, 1)

            norm_one(0, 0)
            low(0, 0)

            def gates(q):
                k = [0]

                def step(ins):
                    k[0] += 1
                    ins.then_inc(gate, 1)
                    dve.wait_ge(gate, q * GATE + k[0])

                dve.wait_ge(r_pe, q + 1)
                rb4 = rbias[:].unsqueeze(1).to_broadcast([C, TT, E])
                step(nc.vector.tensor_tensor(lg[:], lnv_ps[:, 0:TT * E].rearrange("p (t e) -> p t e", t=TT), rb4, ALU.add))
                lj = lg[:].unsqueeze(2).to_broadcast([C, TT, E, E])
                li = lg[:].unsqueeze(3).to_broadcast([C, TT, E, E])
                step(nc.vector.tensor_tensor(ge[:], lj, li, ALU.is_ge))
                step(nc.vector.tensor_tensor(gel[:], ge[:], before[:].unsqueeze(1).to_broadcast([C, TT, E, E]), ALU.mult))
                nc.vector.tensor_reduce(r1[:], gel[:], AX.X, ALU.add).then_inc(gate, 1)
                k[0] += 1
                step(nc.vector.tensor_reduce(r2[:], gel[:].rearrange("p t i j -> p t j i"), AX.X, ALU.add))
                step(nc.vector.tensor_tensor(rank[:], r1[:], r2[:], ALU.subtract))
                step(nc.vector.tensor_tensor(pick[:], rank[:], place_i[:].unsqueeze(1).to_broadcast([C, TT, E]), ALU.is_lt))
                step(nc.vector.tensor_tensor(sl[:], pick[:], lg[:], ALU.mult))
                nc.vector.tensor_reduce(ssum[:], sl[:], AX.X, ALU.add).then_inc(g16_dve, 1)
                dve.wait_ge(g16_dve, 2 * q + 1)
                nc.vector.scalar_tensor_tensor(out=dl[:], in0=ssum[:].unsqueeze(2).to_broadcast([C, TT, E]),
                                               scalar=-0.5, in1=lg[:], op0=ALU.mult, op1=ALU.add).then_inc(gate, 1)

            def gates_end(q):
                dve.wait_ge(th_act, q + 1)
                nc.vector.tensor_scalar(g1[:], th[:], 0.5, 0.5, ALU.mult, ALU.add).then_inc(gate, 1)
                dve.wait_ge(gate, q * GATE + 10)
                nc.vector.tensor_tensor(g2[:], g1[:], pick[:], ALU.mult).then_inc(gate, 1)
                dve.wait_ge(gate, q * GATE + 11)
                nc.vector.tensor_copy(ghr[:], g2[:]).then_inc(gate, 1)
                dve.wait_ge(gate, q * GATE + 12)
                nc.vector.tensor_copy(g16[:, :, 0:E], ghr[:].bitcast(F32))
                nc.vector.tensor_tensor(g16[:, :, E:2 * E], g2[:], ghr[:].bitcast(F32), ALU.subtract).then_inc(g16_dve, 1)

            def rows_end(n):
                dve.wait_ge(b_act, n + 1)
                at_least(dve, bc_pe, n * HEADS)
                nc.vector.tensor_scalar(zr[:, 0, :], b_r[:], low_rows[:], None, ALU.mult).then_inc(rows_dve, 1)
                nc.vector.tensor_scalar(a_r[:], b_r[:], -1.0, 1.0, ALU.mult, ALU.add).then_inc(rows_dve, 1)
                dve.wait_ge(rows_dve, n * ROWS + 2)
                nc.vector.tensor_tensor(new_w[:], b_r[:], zr[:, 0, :].bitcast(F32), ALU.subtract).then_inc(rows_dve, 1)
                nc.vector.tensor_scalar(zr[:, 1, :], a_r[:], low_rows[:], None, ALU.mult).then_inc(rows_dve, 1)
                dve.wait_ge(rows_dve, n * ROWS + 4)
                nc.vector.tensor_tensor(old_w[:], a_r[:], zr[:, 1, :].bitcast(F32), ALU.subtract).then_inc(rows_dve, 1)

            def it(n, p, keys, values, experts, norm, new_rows, new_values):
                v, q = n - 1, n - 2
                if values:
                    rows_end(v)
                if experts:
                    gates(q)
                if values:
                    for h in range(HEADS):
                        dve.wait_ge(v_act, v * HEADS + (h + 1))
                        dve.wait_ge(bc_pe, v * HEADS + (h + 1))
                        at_least(dve, y_dve, v * HEADS + (h - 1))
                        nc.vector.tensor_tensor(z[:, h % 2, :], bc_ps[:, 0, :], sv[:, h % 3, :], ALU.mult).then_inc(z_dve, 1)
                        dve.wait_ge(z_dve, v * HEADS + (h + 1))
                        if h == 0:
                            at_least(dve, acc_pool, v * (HEADS - 1))
                        nc.vector.tensor_tensor_scan(y[:, h, :], bc_ps[:, 1, :], z[:, h % 2, :],
                                                     0.0 if new_values else y[:, h, TOK - 1:TOK],
                                                     ALU.mult, ALU.add).then_inc(y_dve, 1)
                        if h == 1 and experts:
                            gates_end(q)
                elif experts:
                    gates_end(q)

                def expert(e):
                    if experts:
                        dve.wait_ge(g_pe, q * E + (e + 1))
                        if e >= 3:
                            dve.wait_ge(x_pe, q * E + (e - 2))
                        nc.vector.tensor_tensor(xg[:, e % 3, :], bc_ps[:, e % 2, :], xn2[:, p, :], ALU.mult).then_inc(xg_dve, 1)

                expert(0)
                if keys:
                    dve.wait_ge(s_pe, n + 1)
                    at_least(dve, m_dve, n)
                    nc.vector.tensor_tensor_scan(m_r[:], row_ps[:], zeros[:],
                                                 LOWEST if new_rows else m_r[:, TOK - 1:TOK],
                                                 ALU.max, ALU.add).then_inc(m_dve, 1)
                    dve.wait_ge(m_dve, n + 1)
                    at_least(dve, l_dve, n)
                    nc.vector.tensor_tensor(d_r[:], row_ps[:], m_r[:], ALU.subtract).then_inc(d_dve, 1)
                expert(1)
                expert(2)
                if values:
                    dve.wait_ge(acc_pool, v * (HEADS - 1) + (HEADS - 1))
                    tv = t[:, tok(v)]
                    nc.vector.scalar_tensor_tensor(out=tv, in0=acc[:], scalar=1.0 / HEADS, in1=tv, op0=ALU.mult,
                                                   op1=ALU.add).then_inc(t2_dve, 1)
                if keys:
                    dve.wait_ge(e_act, n + 1)
                    at_least(dve, u_dve, n)
                    nc.vector.tensor_tensor_scan(u_r[:], e_r[:], zeros[:], 0.0 if new_rows else u_r[:, TOK - 1:TOK],
                                                 ALU.add, ALU.add).then_inc(u_dve, 1)
                expert(3)
                if norm:
                    norm_one(n + 1, 1 - p)
                expert(4)
                if keys:
                    dve.wait_ge(lu_act, n + 1)
                    nc.vector.tensor_tensor(e_r[:], d_r[:], l_r[:], ALU.subtract).then_inc(l_dve, 1)
                if norm:
                    low(n + 1, 1 - p)
                expert(5)
                expert(6)
                expert(7)
                if values:
                    dve.wait_ge(rs2, v + 1)
                    nc.vector.tensor_tensor(xn2[:, 1 - p, :], lnd_ps[:], ln_r[:], ALU.mult).then_inc(xn2_dve, 1)
                if experts:
                    dve.wait_ge(x_pe, q * E + E)
                    tq = t[:, tok(q)]
                    nc.vector.tensor_tensor(tq, mo_ps[:], tq, ALU.add).then_inc(out_dve, 1)

            walk(dve, it)


def hybrid_layers(nc, x, norm_w, norm_b, Wq, bq, Wk, bk, Wv, bv, Wo, bo, W_kv, q_proj, router_w, router_b,
                  expert_w, expert_b, out):
    B, _, H, W = x.shape
    t_dram = nc.dram_tensor("tokens", (C, B * H * W), F32, kind="Internal").ap()
    softmax_attention(nc, x, norm_w, norm_b, Wq, bq, Wk, bk, Wv, bv, Wo, bo, t_dram)
    scan_attention_and_experts(nc, t_dram, W_kv, q_proj, router_w, router_b, expert_w, expert_b, out)


_INS = ['x', 'L0_conv_norm_w', 'L0_conv_norm_b', 'L0_conv_Wq', 'L0_conv_bq', 'L0_conv_Wk', 'L0_conv_bk',
        'L0_conv_Wv', 'L0_conv_bv', 'L0_conv_Wo', 'L0_conv_bo', 'L1_attn_W_kv', 'L1_attn_q_proj',
        'L1_ffn_router_w', 'L1_ffn_router_b', 'L1_ffn_expert_w', 'L1_ffn_expert_b']
_OUTS = [((4, 128, 64, 64), 'float32')]


def kernel(**inputs):
    import numpy as _np
    import concourse.bacc as _bacc
    from concourse import mybir as _mybir
    from concourse.bass_utils import run_bass_kernel_spmd as _run

    nc = _bacc.Bacc("TRN2", target_bir_lowering=False, num_devices=1)
    arrays, args = {}, []
    for name in _INS:
        a = _np.ascontiguousarray(inputs[name])
        arrays[f"in_{name}_dram"] = a
        args.append(nc.dram_tensor(f"in_{name}_dram", a.shape, _mybir.dt.from_np(a.dtype), kind="ExternalInput").ap())
    for i, (shape, dtype) in enumerate(_OUTS):
        dt = _mybir.dt.from_np(_np.dtype(dtype))
        args.append(nc.dram_tensor(f"out_{i}_dram", shape, dt, kind="ExternalOutput").ap())
    hybrid_layers(nc, *args)
    r = _run(nc, [arrays], core_ids=[0])
    got = tuple(r.results[0][f"out_{i}_dram"] for i in range(len(_OUTS)))
    return got[0]
```

```python
from contextlib import ExitStack

import concourse.bass as bass
from concourse import mybir

F32 = mybir.dt.float32
F32R = mybir.dt.float32r
ALU = mybir.AluOpType
ACT = mybir.ActivationFunctionType
AX = mybir.AxisListType
ds = bass.ds

C = 128
BANK = 512
QB = 256
QT = QB // C
GROUPS = 32
EPS = 1e-5


def softmax_attention(nc, x, norm_w, norm_b, Wq, bq, Wk, bk, Wv, bv, Wo, bo, t_dram):
    B, _, H, W = x.shape
    N = H * W
    NB = N // QB
    KT = N // C
    STEPS = KT // 2
    KCH = N // BANK
    CH = QT * KCH
    XCH = KCH
    XW = N // XCH
    NCH = 4
    NW = N // NCH
    SCALE = float(C) ** -0.5
    AHEAD = 2
    LAG = 2
    RING = 4
    x_v = x.rearrange("b c h w -> b c (h w)")

    with ExitStack() as ctx:
        def sb(name, shape, dt=F32):
            return ctx.enter_context(nc.sbuf_tensor(name, shape, dt))

        def sem(name):
            return ctx.enter_context(nc.semaphore(name))

        xb = sb("xb", [C, 2, N])
        hn = sb("hn", [C, N])
        k_hi, k_lo = sb("k_hi", [C, N], F32R), sb("k_lo", [C, N], F32R)
        v_hi, v_lo = sb("v_hi", [C, KT, C], F32R), sb("v_lo", [C, KT, C], F32R)
        s_sb = sb("s_sb", [C, 2, QT, N])
        q_hi, q_lo = sb("q_hi", [C, 2, QB], F32R), sb("q_lo", [C, 2, QB], F32R)
        pt_hi, pt_lo = sb("pt_hi", [C, RING, 2, QB], F32R), sb("pt_lo", [C, RING, 2, QB], F32R)
        wq, wk, wv, wo = (sb(n, [C, C]) for n in ("wq", "wk", "wv", "wo"))
        wvo, wvT = sb("wvo", [C, C]), sb("wvT", [C, C])
        ident, gavg = sb("ident", [C, C]), sb("gavg", [C, C])
        cols = sb("cols", [C, 6])
        gnw, gnb, bqc, bkc, bvc, boc = (cols[:, i:i + 1] for i in range(6))
        bvo = sb("bvo", [C, 1])
        bn = sb("bn", [C, KCH, 6])
        mom = sb("mom", [C, 2])
        gst = sb("gst", [C, 8])
        ga, gb = sb("ga", [C, 1]), sb("gb", [C, 1])
        gtmp = sb("gtmp", [C, 1])
        epsc = sb("epsc", [C, 1])
        mx = sb("mx", [C, 2, QT, KCH])
        nmax = sb("nmax", [C, 2, QT])
        rsum = sb("rsum", [C, 2, QT, XCH])
        rden = sb("rden", [C, 2, QT])
        rinv = sb("rinv", [C, 2, QT])
        rb_sb = sb("rb_sb", [C, QB])
        on = sb("on", [C, QB])

        s_ps = ctx.enter_context(nc.psum_tensor("s_ps", [C, 2, BANK], F32))
        pt_ps = ctx.enter_context(nc.psum_tensor("pt_ps", [C, RING, 2, QB], F32))
        om_ps = ctx.enter_context(nc.psum_tensor("om_ps", [C, 2, BANK], F32))

        w_in, x_in, t_out = sem("w_in"), sem("x_in"), sem("t_out")
        const_a, const_b = sem("const_a"), sem("const_b")
        wt_pe, wt_cp, wp_pe, wp_cp = sem("wt_pe"), sem("wt_cp"), sem("wp_pe"), sem("wp_cp")
        bn_done, gn_step, gn_tmp = sem("bn_done"), sem("gn_step"), sem("gn_tmp")
        gn_pe, gn_ln, gn_rs = sem("gn_pe"), sem("gn_ln"), sem("gn_rs")
        h_done = sem("h_done")
        kp_pe, k_h, k_l = sem("kp_pe"), sem("k_h"), sem("k_l")
        vp_pe, v_h, v_l = sem("vp_pe"), sem("v_h"), sem("v_l")
        q_pe, q_h, q_l = sem("q_pe"), sem("q_h"), sem("q_l")
        sc_pe, sc_cp, mx_done = sem("sc_pe"), sem("sc_cp"), sem("mx_done")
        exp_done = sem("exp_done")
        tr_pe, p_hi, p_lo, pv_pe = sem("tr_pe"), sem("p_hi"), sem("p_lo"), sem("pv_pe")
        den_done, inv_done, rb_pe, rb_cp = sem("den_done"), sem("inv_done"), sem("rb_pe"), sem("rb_cp")
        on_done, t_done = sem("on_done"), sem("t_done")

        VG = KT // 4
        BN = KCH + 3
        Q_AT, RB_AT = 5, 11
        X_EARLY = 2
        X_LATE = XCH - X_EARLY
        Q2_AT, RB_LAST = 9, 13

        block = ctx.enter_context(nc.Block())

        def walk(eng, prepare, lead, blk):
            def image(b, more):
                lead(b)
                for p in range(2):
                    blk(b, b * NB + p, p, p)
                with eng.Fori(1, NB // 2 - 1) as j:
                    for p in range(2):
                        blk(b, b * NB + j * 2 + p, j * 2 + p, p, pair=j if more else None)
                for p in range(2):
                    blk(b, b * NB + (NB - 2 + p), NB - 2 + p, p, nxt=b + 1 if more else None)

            prepare()
            with eng.Fori(0, B - 1) as b:
                image(b, True)
            image(B - 1, False)

        def is_at(at, *places):
            return isinstance(at, int) and at in places

        @block.sync
        def _(sp):
            for c in range(2):
                sp.dma_start(xb[:, 0, c * N // 2:(c + 1) * N // 2], x_v[0, :, c * N // 2:(c + 1) * N // 2]).then_inc(x_in, 16)
            for t, d in ((wq, Wq), (wk, Wk), (wv, Wv), (wo, Wo)):
                sp.dma_start(t[:], d).then_inc(w_in, 16)
            for i, d in enumerate((norm_w, norm_b, bq, bk, bv, bo)):
                sp.dma_start(cols[:, i:i + 1], d.rearrange("(c o) -> c o", o=1)).then_inc(w_in, 16)
            for b in range(B):
                if b + 1 < B:
                    sp.wait_ge(x_in, 32 * (b + 1))
                    if b >= 1:
                        sp.wait_ge(t_out, 16 * b * NB // 2)
                    for c in range(2):
                        sp.dma_start(xb[:, (b + 1) % 2, c * N // 2:(c + 1) * N // 2],
                                     x_v[b + 1, :, c * N // 2:(c + 1) * N // 2]).then_inc(x_in, 16)
                with sp.Fori(0, NB // 2) as j:
                    sp.wait_ge(t_done, (j * 2) + (b * NB + 2))
                    sp.dma_start(t_dram[:, ds(j * BANK + b * N, BANK)],
                                 xb[:, b % 2, ds(j * BANK, BANK)]).then_inc(t_out, 16)
            sp.wait_ge(t_out, 16 * B * NB // 2)

        @block.gpsimd
        def _(pool):
            nc.gpsimd.memset(ident[:], 0.0).then_inc(const_a, 1)
            nc.gpsimd.memset(gavg[:], float(GROUPS) / C).then_inc(const_a, 1)
            nc.gpsimd.memset(epsc[:], EPS).then_inc(const_b, 1)
            pool.wait_ge(const_a, 2)
            nc.gpsimd.affine_select(out=ident[:], in_=ident[:], compare_op=ALU.not_equal, fill=1.0, base=0,
                                    pattern=[[-1, C]], channel_multiplier=1).then_inc(const_b, 1)
            per = C // GROUPS
            gv = gavg[:].rearrange("p (g c) -> p g c", c=per)
            nc.gpsimd.affine_select(out=gv, in_=gv, compare_op=ALU.is_ge, fill=0.0, base=0,
                                    pattern=[[-per, GROUPS], [0, per]], channel_multiplier=1).then_inc(const_a, 1)
            pool.wait_ge(const_a, 3)
            nc.gpsimd.affine_select(out=gv, in_=gv, compare_op=ALU.is_ge, fill=0.0, base=per - 1,
                                    pattern=[[per, GROUPS], [0, per]], channel_multiplier=-1).then_inc(const_b, 1)

        @block.tensor
        def _(pe):
            def group_means(b, bank):
                pe.wait_ge(gn_step, b * 4 + 1)
                pe.matmul(om_ps[:, bank, 0:2], gavg[:], mom[:], start=True, stop=True).then_inc(gn_pe, 1)

            def project_q(at, bank):
                pe.matmul(om_ps[:, bank, 0:QB], wq[:], hn[:, ds(at * QB, QB)] if not isinstance(at, int)
                          else hn[:, at * QB:(at + 1) * QB], start=True, stop=True).then_inc(q_pe, 1)

            def project_k(b, g):
                if g % 2 == 0:
                    pe.wait_ge(h_done, b * NCH + (g // 2 + 1))
                if g >= 2:
                    pe.wait_ge(k_l, b * KCH + (g - 1))
                pe.matmul(s_ps[:, g % 2, :], wk[:], hn[:, g * BANK:(g + 1) * BANK],
                          start=True, stop=True).then_inc(kp_pe, 1)

            def project_v(b, g):
                if g >= RING:
                    pe.wait_ge(v_l, b * VG + (g - RING + 1))
                dst = pt_ps[:, g % RING, :, :].rearrange("p k q -> p (k q)")
                for i in range(4):
                    kt = g * 4 + i
                    mm = pe.matmul(dst[:, i * C:(i + 1) * C], hn[:, kt * C:(kt + 1) * C], wvo[:],
                                   start=True, stop=True)
                mm.then_inc(vp_pe, 1)

            def scores(n, par, c, first):
                qt, kc = divmod(c, KCH)
                if c == 0:
                    pe.wait_ge(q_l, n + 1)
                if not (first and c < 2):
                    pe.wait_ge(sc_cp, n * CH + (c - 1))
                qs, ks = slice(qt * C, (qt + 1) * C), slice(kc * BANK, (kc + 1) * BANK)
                dst = s_ps[:, c % 2, :]
                pe.matmul(dst, q_hi[:, par, qs], k_hi[:, ks], start=True, stop=False)
                pe.matmul(dst, q_hi[:, par, qs], k_lo[:, ks], start=False, stop=False)
                pe.matmul(dst, q_lo[:, par, qs], k_hi[:, ks], start=False, stop=True).then_inc(sc_pe, 1)

            def turn(n, par, s, first):
                if s % (STEPS // XCH) == 0:
                    pe.wait_ge(exp_done, n * 2 * XCH + (XCH + s // (STEPS // XCH) + 1))
                if not (first and s < RING):
                    pe.wait_ge(p_lo, n * STEPS + (s - RING + 1))
                for k in range(2):
                    for qt in range(QT):
                        kt = 2 * s + k
                        mm = pe.transpose(pt_ps[:, s % RING, k, qt * C:(qt + 1) * C],
                                          s_sb[:, par, qt, kt * C:(kt + 1) * C], ident[:])
                mm.then_inc(tr_pe, 1)

            def weigh(n, par, s, at):
                pe.wait_ge(p_lo, n * STEPS + (s + 1))
                if s == 0 and not is_at(at, 0):
                    pe.wait_ge(rb_cp, n)
                if s == 0 and not is_at(at, 0, 1):
                    pe.wait_ge(on_done, n - 1)
                o = om_ps[:, par, 0:QB]
                for k in range(2):
                    kt = 2 * s + k
                    pe.matmul(o, v_hi[:, kt, :], pt_hi[:, s % RING, k, :], start=(kt == 0), stop=False)
                    pe.matmul(o, v_lo[:, kt, :], pt_hi[:, s % RING, k, :], start=False, stop=False)
                    mm = pe.matmul(o, v_hi[:, kt, :], pt_lo[:, s % RING, k, :], start=False, stop=(kt == KT - 1))
                mm.then_inc(pv_pe, 1)

            def spread_sums(n, p):
                pe.wait_ge(inv_done, n + 1)
                for qt in range(QT):
                    mm = pe.matmul(om_ps[:, 1 - p, qt * C:(qt + 1) * C],
                                   rinv[:, p, qt:qt + 1].to_broadcast([C, C]), ident[:], start=True, stop=True)
                mm.then_inc(rb_pe, 1)

            def prepare():
                pe.wait_ge(w_in, 160)
                pe.wait_ge(const_b, 3)
                pe.transpose(om_ps[:, 0, 0:C], wv[:], ident[:]).then_inc(wt_pe, 1)
                pe.wait_ge(wt_cp, 1)
                pe.matmul(om_ps[:, 0, 0:C], wvT[:], wo[:], start=True, stop=True)
                pe.matmul(om_ps[:, 0, C:C + 1], wo[:], bvc, start=True, stop=True).then_inc(wp_pe, 1)
                group_means(0, 1)
                pe.wait_ge(wp_cp, 2)
                pe.wait_ge(h_done, 1)
                project_q(0, 0)
                for g in range(KCH):
                    project_k(0, g)
                    if g == 1:
                        pe.wait_ge(q_l, 1)
                        project_q(1, 0)

            def lead(b):
                pe.wait_ge(k_l, b * KCH + KCH)
                for c in range(CH):
                    scores(b * NB, 0, c, True)
                    if c % 2:
                        project_v(b, c // 2)
                pe.wait_ge(v_l, b * VG + VG)

            def blk(b, n, at, p, nxt=None, pair=None):
                first, last = is_at(at, 0), is_at(at, NB - 1)
                ends = is_at(at, NB - 2, NB - 1)
                for c in range(AHEAD):
                    if not last:
                        scores(n + 1, 1 - p, c, False)
                for s in range(STEPS):
                    turn(n, p, s, first)
                    if not last and s + AHEAD < CH:
                        scores(n + 1, 1 - p, s + AHEAD, False)
                    if last and nxt is not None and s % 2 == 0:
                        if s < 4:
                            pe.wait_ge(sc_cp, n * CH + (CH - 1 + s // 2))
                        project_k(nxt, s // 2)
                    if s >= LAG:
                        weigh(n, p, s - LAG, at)
                    elif not first:
                        weigh(n - 1, 1 - p, STEPS - LAG + s, None)
                    if s == Q_AT and not first:
                        pe.wait_ge(on_done, n)
                    if s == Q_AT and not ends:
                        project_q(at + 2, 1 - p)
                    if nxt is not None and is_at(at, NB - 2) and s == Q_AT:
                        group_means(nxt, 1 - p)
                    if nxt is not None and last and s == Q_AT:
                        project_q(0, 1 - p)
                    if nxt is not None and last and s == Q2_AT:
                        pe.wait_ge(q_l, n + 2)
                        project_q(1, 1 - p)
                    if s == (RB_LAST if last else RB_AT):
                        if not ends:
                            pe.wait_ge(q_l, n + 3)
                        elif nxt is not None and last:
                            pe.wait_ge(q_l, n + 3)
                        elif nxt is not None:
                            pe.wait_ge(gn_step, nxt * 4 + 2)
                        spread_sums(n, p)
                if last:
                    for s in range(STEPS - LAG, STEPS):
                        weigh(n, p, s, at)

            walk(pe, prepare, lead, blk)

        @block.scalar
        def _(act):
            def split_q(n, par, bank):
                act.wait_ge(q_pe, n + 1)
                nc.scalar.activation(q_hi[:, par, :], om_ps[:, bank, 0:QB], ACT.Identity, bias=bqc).then_inc(q_h, 1)

            def split_k(b, g):
                act.wait_ge(kp_pe, b * KCH + (g + 1))
                nc.scalar.activation(k_hi[:, g * BANK:(g + 1) * BANK], s_ps[:, g % 2, :], ACT.Identity,
                                     bias=bkc).then_inc(k_h, 1)

            def exps(n, par, qt, c):
                if c == 0:
                    act.wait_ge(mx_done, n * QT + (qt + 1))
                sl = s_sb[:, par, qt, c * XW:(c + 1) * XW]
                nc.scalar.activation(sl, sl, ACT.Exp, bias=nmax[:, par, qt:qt + 1],
                                     accum_out=rsum[:, par, qt, c:c + 1]).then_inc(exp_done, 1)

            def group_scale(b):
                act.wait_ge(gn_step, b * 4 + 3)
                nc.scalar.activation(gst[:, 4:5], gst[:, 3:4], ACT.Ln, bias=epsc[:]).then_inc(gn_ln, 1)
                act.wait_ge(gn_ln, b + 1)
                nc.scalar.activation(gst[:, 5:6], gst[:, 4:5], ACT.Exp, scale=-0.5).then_inc(gn_rs, 1)

            def normalise(b, c):
                if c == 0:
                    act.wait_ge(gn_step, b * 4 + 4)
                xs = xb[:, b % 2 if isinstance(b, int) else ds(b % 2, 1), c * NW:(c + 1) * NW]
                nc.scalar.activation(hn[:, c * NW:(c + 1) * NW], xs, ACT.Identity, bias=gb[:],
                                     scale=ga[:]).then_inc(h_done, 1)

            def prepare():
                nc.scalar.preload_act_table_set("natural_log_exp_and_others")
                act.wait_ge(wt_pe, 1)
                nc.scalar.copy(wvT[:], om_ps[:, 0, 0:C]).then_inc(wt_cp, 1)
                act.wait_ge(wp_pe, 1)
                nc.scalar.copy(wvo[:], om_ps[:, 0, 0:C]).then_inc(wp_cp, 1)
                group_scale(0)
                for c in range(NCH):
                    normalise(0, c)
                    if c == 0:
                        split_q(0, 0, 0)
                for g in range(KCH):
                    split_k(0, g)
                    if g == 1:
                        split_q(1, 1, 0)

            def lead(b):
                for g in range(VG):
                    act.wait_ge(vp_pe, b * VG + (g + 1))
                    nc.scalar.copy(v_hi[:, g * 4:g * 4 + 4, :].rearrange("p a c -> p (a c)"),
                                   pt_ps[:, g % RING, :, :].rearrange("p k q -> p (k q)")).then_inc(v_h, 1)
                    if g >= VG // 2:
                        for c in range(2):
                            exps(b * NB, 0, 0, (g - VG // 2) * 2 + c)
                for c in range(X_EARLY):
                    exps(b * NB, 0, 1, c)

            def blk(b, n, at, p, nxt=None, pair=None):
                first, last = is_at(at, 0), is_at(at, NB - 1)
                ends = is_at(at, NB - 2, NB - 1)
                for s in range(STEPS):
                    act.wait_ge(tr_pe, n * STEPS + (s + 1))
                    if not (first and s < RING):
                        act.wait_ge(pv_pe, n * STEPS + (s - RING + 1))
                    nc.scalar.copy(pt_hi[:, s % RING, :, :], pt_ps[:, s % RING, :, :]).then_inc(p_hi, 1)
                    if s < X_LATE:
                        exps(n, p, 1, X_EARLY + s)
                    elif not last:
                        exps(n + 1, 1 - p, (s - X_LATE) // XCH, (s - X_LATE) % XCH)
                    if nxt is not None and is_at(at, NB - 2):
                        if s == Q_AT + 1:
                            group_scale(nxt)
                        if s in (9, 11, 13, 15):
                            normalise(nxt, (s - 9) // 2)
                    if nxt is not None and last:
                        if s % 2:
                            split_k(nxt, s // 2)
                        if s == Q_AT + 1:
                            split_q(n + 1, 0, 1 - p)
                        if s == Q2_AT + 1:
                            split_q(n + 2, 1, 1 - p)
                    if s == Q_AT and not ends:
                        split_q(n + 2, p, 1 - p)
                    if s == (RB_LAST if last else RB_AT):
                        act.wait_ge(rb_pe, n + 1)
                        if not first:
                            act.wait_ge(on_done, n)
                        nc.scalar.copy(rb_sb[:], om_ps[:, 1 - p, 0:QB]).then_inc(rb_cp, 1)

            walk(act, prepare, lead, blk)

        @block.vector
        def _(dve):
            def split_q(n, par, bank):
                dve.wait_ge(q_h, n + 1)
                nc.vector.scalar_tensor_tensor(out=q_lo[:, par, :], in0=om_ps[:, bank, 0:QB], scalar=bqc,
                                               in1=q_hi[:, par, :].bitcast(F32), op0=ALU.add,
                                               op1=ALU.subtract).then_inc(q_l, 1)

            def split_k(b, g):
                dve.wait_ge(k_h, b * KCH + (g + 1))
                sl = slice(g * BANK, (g + 1) * BANK)
                nc.vector.scalar_tensor_tensor(out=k_lo[:, sl], in0=s_ps[:, g % 2, :], scalar=bkc,
                                               in1=k_hi[:, sl].bitcast(F32), op0=ALU.add,
                                               op1=ALU.subtract).then_inc(k_l, 1)

            def score_copy(n, par, c):
                qt, kc = divmod(c, KCH)
                dve.wait_ge(sc_pe, n * CH + (c + 1))
                nc.vector.tensor_scalar(s_sb[:, par, qt, kc * BANK:(kc + 1) * BANK], s_ps[:, c % 2, :],
                                        SCALE, None, ALU.mult, ALU.max,
                                        accum_out=mx[:, par, qt, kc:kc + 1]).then_inc(sc_cp, 1)
                if kc == KCH - 1:
                    dve.wait_ge(sc_cp, n * CH + (c + 1))
                    nc.vector.tensor_reduce(nmax[:, par, qt:qt + 1], mx[:, par, qt, :], AX.X, ALU.max,
                                            negate=True).then_inc(mx_done, 1)

            def finish(n, at, par, bpar):
                dve.wait_ge(pv_pe, n * STEPS + STEPS)
                dve.wait_ge(rb_cp, n + 1)
                nc.vector.tensor_tensor(on[:], om_ps[:, par, 0:QB], rb_sb[:], ALU.mult).then_inc(on_done, 1)
                dve.wait_ge(on_done, n + 1)
                xs = xb[:, ds(bpar, 1), ds(at * QB, QB)].rearrange("c o n -> c (o n)")
                nc.vector.scalar_tensor_tensor(out=xs, in0=on[:], scalar=bvo[:], in1=xs, op0=ALU.add,
                                               op1=ALU.add).then_inc(t_done, 1)

            def moments(b, c):
                xs = xb[:, b % 2 if isinstance(b, int) else ds(b % 2, 1),
                        c * BANK:(c + 1) * BANK] if isinstance(c, int) else xb[:, ds(b % 2, 1), ds(c * BANK, BANK)]
                dst = bn[:, c, :] if isinstance(c, int) else bn[:, ds(c, 1), :]
                nc.vector.bn_stats(dst, xs).then_inc(bn_done, 1)

            def channel_moments(b):
                dve.wait_ge(bn_done, b * BN + KCH)
                nc.vector.memset(gst[:, 6:7], 0.0)
                nc.vector.bn_aggr(mom[:], bn[:].rearrange("p a s -> p (a s)")).then_inc(bn_done, 1)
                dve.wait_ge(bn_done, b * BN + (KCH + 1))
                nc.vector.tensor_tensor(gtmp[:], mom[:, 0:1], mom[:, 0:1], ALU.mult).then_inc(bn_done, 1)
                dve.wait_ge(bn_done, b * BN + (KCH + 2))
                nc.vector.tensor_tensor(mom[:, 1:2], mom[:, 1:2], gtmp[:], ALU.add).then_inc(gn_step, 1)

            def group_variance(b, bank):
                dve.wait_ge(gn_pe, b + 1)
                nc.vector.tensor_copy(gst[:, 0:2], om_ps[:, bank, 0:2]).then_inc(gn_step, 1)
                dve.wait_ge(gn_step, b * 4 + 2)
                nc.vector.scalar_tensor_tensor(out=gst[:, 2:3], in0=gst[:, 0:1], scalar=gst[:, 0:1],
                                               in1=gst[:, 1:2], op0=ALU.mult, op1=ALU.subtract).then_inc(gn_tmp, 1)
                dve.wait_ge(gn_tmp, b * 2 + 1)
                nc.vector.tensor_scalar(gst[:, 3:4], gst[:, 2:3], -1.0, 0.0, ALU.mult, ALU.max).then_inc(gn_step, 1)

            def scale_shift(b):
                dve.wait_ge(gn_rs, b + 1)
                nc.vector.tensor_tensor(ga[:], gst[:, 5:6], gnw, ALU.mult).then_inc(gn_tmp, 1)
                dve.wait_ge(gn_tmp, b * 2 + 2)
                nc.vector.tensor_tensor(gtmp[:], gst[:, 0:1], ga[:], ALU.mult).then_inc(bn_done, 1)
                dve.wait_ge(bn_done, b * BN + BN)
                nc.vector.tensor_tensor(gb[:], gnb, gtmp[:], ALU.subtract).then_inc(gn_step, 1)

            def prepare():
                dve.wait_ge(x_in, 32)
                for c in range(KCH):
                    moments(0, c)
                channel_moments(0)
                dve.wait_ge(wp_pe, 1)
                dve.wait_ge(wp_cp, 1)
                nc.vector.tensor_tensor(bvo[:], om_ps[:, 0, C:C + 1], boc, ALU.add).then_inc(wp_cp, 1)
                group_variance(0, 1)
                scale_shift(0)
                split_q(0, 0, 0)
                for g in range(KCH):
                    split_k(0, g)
                    if g == 1:
                        split_q(1, 1, 0)

            def lead(b):
                for c in range(CH):
                    score_copy(b * NB, 0, c)
                    if c % 2:
                        g = c // 2
                        dve.wait_ge(v_h, b * VG + (g + 1))
                        dst = slice(g * 4, g * 4 + 4)
                        nc.vector.tensor_tensor(v_lo[:, dst, :].rearrange("p a c -> p (a c)"),
                                                pt_ps[:, g % RING, :, :].rearrange("p k q -> p (k q)"),
                                                v_hi[:, dst, :].rearrange("p a c -> p (a c)").bitcast(F32),
                                                ALU.subtract).then_inc(v_l, 1)

            def blk(b, n, at, p, nxt=None, pair=None):
                first, last = is_at(at, 0), is_at(at, NB - 1)
                ends = is_at(at, NB - 2, NB - 1)
                if not last:
                    for c in range(AHEAD - 1):
                        score_copy(n + 1, 1 - p, c)
                for s in range(STEPS):
                    if pair is not None and p == 0 and s == 1 or nxt is not None and is_at(at, NB - 2) and s == 0:
                        dve.wait_ge(x_in, b * 32 + 64)
                    if not last and s + AHEAD - 1 < CH:
                        score_copy(n + 1, 1 - p, s + AHEAD - 1)
                    dve.wait_ge(p_hi, n * STEPS + (s + 1))
                    nc.vector.tensor_tensor(pt_lo[:, s % RING, :, :], pt_ps[:, s % RING, :, :],
                                            pt_hi[:, s % RING, :, :].bitcast(F32), ALU.subtract).then_inc(p_lo, 1)
                    if s == LAG + 1 and not first:
                        finish(n - 1, at - 1, 1 - p, b % 2)
                    if pair is not None and p == 0 and s == 1:
                        moments(b + 1, pair - 1)
                    if nxt is not None and is_at(at, NB - 2):
                        if s < 2:
                            moments(nxt, KCH - 2 + s)
                        if s == 2:
                            channel_moments(nxt)
                        if s == Q_AT + 1:
                            group_variance(nxt, 1 - p)
                        if s == Q_AT + 2:
                            scale_shift(nxt)
                    if nxt is not None and last:
                        if s % 2:
                            split_k(nxt, s // 2)
                        if s == Q_AT + 2:
                            split_q(n + 1, 0, 1 - p)
                        if s == Q2_AT + 2:
                            split_q(n + 2, 1, 1 - p)
                    if s == Q_AT + 1 and not ends:
                        split_q(n + 2, p, 1 - p)
                    if s == 9:
                        dve.wait_ge(exp_done, n * 2 * XCH + 2 * XCH)
                        nc.vector.tensor_reduce(rden[:, p, :], rsum[:, p, :, :], AX.X, ALU.add).then_inc(den_done, 1)
                        dve.wait_ge(den_done, n + 1)
                        nc.vector.reciprocal(rinv[:, p, :], rden[:, p, :]).then_inc(inv_done, 1)
                if last:
                    finish(n, at, p, b % 2)

            walk(dve, prepare, lead, blk)


def scan_attention_and_experts(nc, t_dram, W_kv, q_proj, router_w, router_b, expert_w, expert_b, out):
    B, _, H, W = out.shape
    N = H * W
    HEADS = q_proj.shape[0]
    E = router_w.shape[1]
    TOK = BANK
    PER = N // TOK
    NBLK = B * PER
    TT = TOK // C
    QUAD, HALF = 32, 16
    LOWEST = -3.0e38
    out_v = out.rearrange("b c h w -> b c (h w)")

    with ExitStack() as ctx:
        def sb(name, shape, dt=F32):
            return ctx.enter_context(nc.sbuf_tensor(name, shape, dt))

        def psum(name, shape):
            return ctx.enter_context(nc.psum_tensor(name, shape, F32))

        def sem(name):
            return ctx.enter_context(nc.semaphore(name))

        t = sb("t", [C, NBLK * TOK])
        w_hi, w_lo = sb("w_hi", [C, HEADS, 2, C], F32R), sb("w_lo", [C, HEADS, 2, C], F32R)
        qcol = sb("qcol", [C, HEADS])
        qz = sb("qz", [C, HEADS, QUAD])
        rw = sb("rw", [C, E])
        rbias = sb("rbias", [C, E])
        ew = sb("ew", [C, E, C])
        eb = sb("eb", [C, C])
        eb_hi, eb_lo = sb("eb_hi", [C, C], F32R), sb("eb_lo", [C, C], F32R)
        ident, center, mean_w = sb("ident1", [C, C]), sb("center", [C, C]), sb("mean_w", [C, C])
        center_r, mean_r = sb("center_r", [C, C], F32R), sb("mean_r", [C, C], F32R)
        sel_h = sb("sel_h", [C, HEADS, C], F32R)
        sel_e = sb("sel_e", [C, E, C], F32R)
        low_rows4, low_rows, neg_low = sb("low_rows4", [C, 4]), sb("low_rows", [C, 1]), sb("neg_low", [C, 1])
        ones = sb("ones", [C, 1])
        before = sb("before", [C, E, E])
        place_i = sb("place_i", [C, E])
        zeros = sb("zeros", [C, TOK])
        epsc = sb("epsc1", [C, 1])

        ln_sq, ln_l, ln_r = sb("ln_sq", [C, TOK]), sb("ln_l", [C, TOK]), sb("ln_r", [C, TOK])
        t_h, t_l = sb("t_h", [C, TOK], F32R), sb("t_l", [C, TOK], F32R)
        ln_sh, ln_sl = sb("ln_sh", [C, TOK], F32R), sb("ln_sl", [C, TOK], F32R)
        xf = sb("xf", [C, TOK])
        xn_hi, xn_lo = sb("xn_hi", [C, 2, TOK], F32R), sb("xn_lo", [C, 2, TOK], F32R)
        xn2 = sb("xn2", [C, 2, TOK])
        sk = sb("sk", [C, HEADS, TOK])
        sv = sb("sv", [C, 3, TOK])
        m_r, d_r, e_r, u_r = (sb(n, [C, TOK]) for n in ("m_r", "d_r", "e_r", "u_r"))
        l_r, b_r, a_r = (sb(n, [C, TOK]) for n in ("l_r", "b_r", "a_r"))
        zr = sb("zr", [C, 2, TOK], F32R)
        new_w, old_w = sb("new_w", [C, TOK], F32R), sb("old_w", [C, TOK], F32R)
        z = sb("z", [C, 2, TOK])
        y = sb("y", [C, HEADS, TOK])
        wkv = y[:, 0:HEADS // 2, :].rearrange("p h (x c) -> p (h x) c", c=C).rearrange(
            "p (h two) c -> p h two c", two=2)
        acc = sb("acc", [C, TOK])
        xg = sb("xg", [C, 3, TOK])
        lg = sb("lg", [C, TT, E])
        ge, gel = sb("ge", [C, TT, E, E]), sb("gel", [C, TT, E, E])
        r1, r2, rank, pick = (sb(n, [C, TT, E]) for n in ("r1", "r2", "rank", "pick"))
        sl, dl, th, g1, g2 = (sb(n, [C, TT, E]) for n in ("sl", "dl", "th", "g1", "g2"))
        ssum = sb("ssum", [C, TT])
        ghr = sb("ghr", [C, TT, E], F32R)
        g16 = sb("g16", [C, TT, 2 * E])
        gt = sb("gt", [C, TOK], F32R)

        kv_ps = psum("kv_ps", [C, 2, BANK])
        bc_ps = psum("bc_ps", [C, 2, BANK])
        row_ps = psum("row_ps", [C, BANK])
        mo_ps = psum("mo_ps", [C, BANK])
        lnd_ps = psum("lnd_ps", [C, BANK])
        lnv_ps = psum("lnv_ps", [C, BANK])

        names = """w_in wkv_in t_in t_out cst1 cst2 cst3 wt_pe wt_hi wt_lo
            k_pe s_pe v_pe bcn_pe bc_pe g_pe x_pe c1_pe w1_pe c2_pe w2_pe r_pe gt_pe
            k_act v_act sq1 sq2 ln1 ln2 rs1 rs2 hi_act e_act lu_act b_act rows_act th_act gt_act
            z_dve y_dve m_dve d_dve u_dve l_dve rows_dve xf_dve xn2_dve xg_dve t2_dve out_dve gate g16_dve
            acc_pool lo_pool
            tk_hi tk_lo sq_hi sq_lo""".split()
        (w_in, wkv_in, t_in, t_out, cst1, cst2, cst3, wt_pe, wt_hi, wt_lo,
         k_pe, s_pe, v_pe, bcn_pe, bc_pe, g_pe, x_pe, c1_pe, w1_pe, c2_pe, w2_pe, r_pe, gt_pe,
         k_act, v_act, sq1, sq2, ln1, ln2, rs1, rs2, hi_act, e_act, lu_act, b_act, rows_act, th_act, gt_act,
         z_dve, y_dve, m_dve, d_dve, u_dve, l_dve, rows_dve, xf_dve, xn2_dve, xg_dve, t2_dve, out_dve,
         gate, g16_dve, acc_pool, lo_pool,
         tk_hi, tk_lo, sq_hi, sq_lo) = (sem(n) for n in names)
        C2_AT, W2_AT = 3, 4
        GATE = 12

        block = ctx.enter_context(nc.Block())

        def at_least(eng, s, value):
            if not (isinstance(value, int) and value <= 0):
                eng.wait_ge(s, value)

        def loaded(eng, n):
            if not isinstance(n, int) or n == 0 or n % PER == PER - 1:
                eng.wait_ge(t_in, 16 * (2 if isinstance(n, int) and n + 1 < PER else B + 1))

        def walk(eng, it):
            def pair(n, first, last=False):
                for p in range(2):
                    it(n + p, p, keys=True, values=not (isinstance(n, int) and n + p < 1),
                       experts=not (isinstance(n, int) and n + p < 2), norm=not (last and p == 1),
                       new_rows=first and p == 0, new_values=first and p == 1)

            pair(0, True)
            with eng.Fori(1, PER // 2) as j:
                pair(j * 2, False)
            with eng.Fori(1, B - 1) as b:
                pair(b * PER, True)
                with eng.Fori(1, PER // 2) as j:
                    pair(b * PER + j * 2, False)
            pair((B - 1) * PER, True)
            with eng.Fori(1, PER // 2 - 1) as j:
                pair(j * 2 + (B - 1) * PER, False)
            pair(NBLK - 2, False, True)
            it(NBLK, 0, keys=False, values=True, experts=True, norm=False, new_rows=False, new_values=False)
            it(NBLK + 1, 1, keys=False, values=False, experts=True, norm=False, new_rows=False, new_values=False)

        def tok(n):
            return slice(n * TOK, (n + 1) * TOK) if isinstance(n, int) else ds(n * TOK, TOK)

        @block.sync
        def _(sp):
            sp.dma_start(t[:, 0:TOK], t_dram[:, 0:TOK]).then_inc(t_in, 16)
            sp.dma_start(wkv, W_kv.rearrange("(h d two) c -> d h two c", h=HEADS, two=2)).then_inc(wkv_in, 16)
            sp.dma_start(qcol[:], q_proj.rearrange("h d -> d h"), allow_slow_non_contiguous=True).then_inc(w_in, 16)
            sp.dma_start(rw[:], router_w).then_inc(w_in, 16)
            sp.dma_start(rbias[:], router_b.rearrange("(o e) -> o e", o=1).to_broadcast([C, E])).then_inc(w_in, 16)
            sp.dma_start(ew[:], expert_w.rearrange("e c d -> c e d")).then_inc(w_in, 16)
            sp.wait_ge(cst2, 1)
            for i in range(2):
                sp.dma_start(eb[i * E:(i + 1) * E, :], expert_b).then_inc(w_in, 16)
            for b in range(B):
                sp.wait_ge(t_in, 16 * (b + 1))
                first = b * N if b else TOK
                sp.dma_start(t[:, first:(b + 1) * N], t_dram[:, first:(b + 1) * N]).then_inc(t_in, 16)
            for b in range(B):
                with sp.Fori(0, PER) as j:
                    sp.wait_ge(out_dve, j + (b * PER + 1))
                    sp.dma_start(out_v[b, :, ds(j * TOK, TOK)], t[:, ds(j * TOK + b * N, TOK)]).then_inc(t_out, 16)
            sp.wait_ge(t_out, 16 * NBLK)

        @block.gpsimd
        def _(pool):
            nc.gpsimd.memset(eb[:], 0.0).then_inc(cst2, 1)
            nc.gpsimd.memset(ident[:], 0.0).then_inc(cst1, 1)
            nc.gpsimd.memset(low_rows4[:], 1.0).then_inc(cst1, 1)
            nc.gpsimd.memset(before[:], 1.0).then_inc(cst1, 1)
            nc.gpsimd.memset(mean_w[:], 1.0 / C).then_inc(cst1, 1)
            nc.gpsimd.memset(epsc[:], EPS).then_inc(cst1, 1)
            nc.gpsimd.memset(zeros[:], 0.0).then_inc(cst1, 1)
            nc.gpsimd.memset(ones[:], 1.0).then_inc(cst1, 1)
            nc.gpsimd.memset(qz[:], 0.0).then_inc(cst1, 1)
            nc.gpsimd.memset(gt[:].bitcast(F32), 0.0).then_inc(cst1, 1)
            pool.wait_ge(cst1, 9)
            nc.gpsimd.affine_select(out=ident[:], in_=ident[:], compare_op=ALU.not_equal, fill=1.0, base=0,
                                    pattern=[[-1, C]], channel_multiplier=1).then_inc(cst3, 1)
            nc.gpsimd.affine_select(out=before[:], in_=before[:], compare_op=ALU.is_gt, fill=0.0, base=0,
                                    pattern=[[1, E], [-1, E]], channel_multiplier=0).then_inc(cst3, 1)
            nc.gpsimd.affine_select(out=low_rows4[:], in_=low_rows4[:], compare_op=ALU.is_ge, fill=0.0, base=-HALF,
                                    pattern=[[-QUAD, 4]], channel_multiplier=1).then_inc(cst1, 1)
            pool.wait_ge(cst1, 10)
            nc.gpsimd.affine_select(out=low_rows4[:], in_=low_rows4[:], compare_op=ALU.is_ge, fill=0.0,
                                    base=QUAD - 1, pattern=[[QUAD, 4]], channel_multiplier=-1).then_inc(cst3, 1)

            def low(n, par):
                pool.wait_ge(hi_act, n + 1)
                nc.gpsimd.tensor_tensor(xn_lo[:, par, :], xf[:], xn_hi[:, par, :].bitcast(F32),
                                        ALU.subtract).then_inc(lo_pool, 1)

            low(0, 0)

            def low_squares(n):
                pool.wait_ge(sq_hi, n + 1)
                nc.gpsimd.tensor_tensor(ln_sl[:], ln_sq[:], ln_sh[:].bitcast(F32), ALU.subtract).then_inc(sq_lo, 1)

            def it(n, p, keys, values, experts, norm, new_rows, new_values):
                if norm:
                    pool.wait_ge(tk_hi, n + 1)
                    nc.gpsimd.tensor_tensor(t_l[:], t[:, tok(n + 1)], t_h[:].bitcast(F32),
                                            ALU.subtract).then_inc(tk_lo, 1)
                if norm and not values:
                    low_squares(n)
                if values:
                    v = n - 1
                    at_least(pool, t2_dve, v)
                    for h in range(1, HEADS):
                        pool.wait_ge(y_dve, v * HEADS + (h + 1))
                        if h > 1:
                            pool.wait_ge(acc_pool, v * (HEADS - 1) + (h - 1))
                        nc.gpsimd.tensor_tensor(acc[:], y[:, 0, :] if h == 1 else acc[:], y[:, h, :],
                                                ALU.add).then_inc(acc_pool, 1)
                        if norm and h == 4:
                            low_squares(n)
                if norm:
                    low(n + 1, 1 - p)

            walk(pool, it)

        @block.tensor
        def _(pe):
            def project(dst, head, two, par):
                pe.matmul(dst, w_hi[:, head, two, :], xn_hi[:, par, :], start=True, stop=False)
                pe.matmul(dst, w_hi[:, head, two, :], xn_lo[:, par, :], start=False, stop=False)
                return pe.matmul(dst, w_lo[:, head, two, :], xn_hi[:, par, :], start=False, stop=True)

            def row_sums(n, j, routed):
                if j == 0:
                    at_least(pe, d_dve, n)
                if routed:
                    pe.wait_ge(gate, (n - 2) * GATE + 1)
                pe.wait_ge(k_act, n * HEADS + (4 * j + 4))
                for g in range(4):
                    h = 4 * j + g
                    mm = pe.matmul(row_ps[QUAD * g:QUAD * (g + 1), :], qz[:, h, :], sk[:, h, :],
                                   start=(j == 0), stop=(j == 1))
                if j == 1:
                    mm.then_inc(s_pe, 1)

            def norm_center(n, s_in, free, s_out):
                if s_in is not None:
                    pe.wait_ge(s_in, n + 1)
                at_least(pe, *free)
                pe.matmul(lnd_ps[:], center[:], t[:, tok(n)], start=True, stop=True).then_inc(s_out, 1)

            def norm_var(n, sq, free, s_out):
                pe.wait_ge(sq, n + 1)
                at_least(pe, *free)
                pe.matmul(lnv_ps[:], mean_w[:], ln_sq[:], start=True, stop=True).then_inc(s_out, 1)

            pe.wait_ge(cst3, 4)
            pe.wait_ge(t_in, 16)
            norm_center(0, None, (xn2_dve, 0), c1_pe)
            norm_var(0, sq1, (ln2, 0), w1_pe)
            pe.wait_ge(wkv_in, 16)
            for g in range(2 * HEADS // TT):
                if g >= 2:
                    pe.wait_ge(wt_lo, g - 1)
                for i in range(TT):
                    h, two = divmod(g * TT + i, 2)
                    mm = pe.transpose(kv_ps[:, g % 2, i * C:(i + 1) * C], wkv[:, h, two, :], ident[:])
                mm.then_inc(wt_pe, 1)
            pe.wait_ge(wt_lo, 2 * HEADS // TT)

            def key(n, p, h, alone):
                if h == 0:
                    pe.wait_ge(lo_pool, n + 1)
                if alone:
                    if h >= 2:
                        pe.wait_ge(k_act, n * HEADS + (h - 1))
                else:
                    pe.wait_ge(k_act, n * HEADS + h)
                project(kv_ps[:, h % 2 if alone else 0, :], h, 0, p).then_inc(k_pe, 1)

            def value(n, p, h, alone):
                v = n - 1
                if h < 2:
                    pe.wait_ge(k_act, n * HEADS)
                if not alone or h < 2:
                    at_least(pe, v_act, v * HEADS + (0 if alone else h))
                else:
                    pe.wait_ge(v_act, v * HEADS + (h - 1))
                project(kv_ps[:, h % 2 if alone else 1, :], h, 1, 1 - p).then_inc(v_pe, 1)

            def new_weight(v, h):
                if h == 0:
                    pe.wait_ge(rows_dve, 2 * v + 1)
                else:
                    pe.wait_ge(z_dve, v * HEADS + h)
                pe.matmul(bc_ps[:, 0, :], sel_h[:, h, :], new_w[:], start=True, stop=True).then_inc(bcn_pe, 1)

            def old_weight(v, h):
                if h == 0:
                    pe.wait_ge(rows_dve, 2 * v + 2)
                else:
                    pe.wait_ge(y_dve, v * HEADS + h)
                pe.matmul(bc_ps[:, 1, :], sel_h[:, h, :], old_w[:], start=True, stop=True).then_inc(bc_pe, 1)

            def it(n, p, keys, values, experts, norm, new_rows, new_values):
                v, q = n - 1, n - 2
                for h in range(-1, HEADS):
                    if values and h > 0:
                        new_weight(v, h)
                    if values and h + 1 < HEADS:
                        value(n, p, h + 1, not keys)
                    if values and h == -1:
                        new_weight(v, 0)
                    if experts and h == HEADS - 1:
                        turn_gates(q)
                    if values and h >= 0:
                        old_weight(v, h)
                    if keys and h + 1 < HEADS:
                        key(n, p, h + 1, not values)
                    if experts and h == -1:
                        router(n, q, p, keys)
                    if norm and h == 2:
                        pe.wait_ge(tk_lo, n + 1)
                        at_least(pe, xn2_dve, n - 1)
                        pe.matmul(lnd_ps[:], center_r[:], t_h[:], start=True, stop=False)
                        pe.matmul(lnd_ps[:], center_r[:], t_l[:], start=False, stop=True).then_inc(c1_pe, 1)
                    if (isinstance(n, int) and n == 0) and h == 5:
                        pe.wait_ge(cst3, 5)
                        pe.wait_ge(w_in, 16 * 6)
                    if keys and h == 5:
                        row_sums(n, 0, experts)
                if keys:
                    row_sums(n, 1, False)
                if experts:
                    pe.wait_ge(gt_act, q + 1)
                    if values:
                        pe.wait_ge(z_dve, v * HEADS + HEADS)
                    spread(q, 0)
                    if values:
                        pe.wait_ge(y_dve, v * HEADS + HEADS)
                    spread(q, 1)
                if norm:
                    pe.wait_ge(sq_lo, n + 1)
                    at_least(pe, ln2, n - 1)
                    pe.matmul(lnv_ps[:], mean_r[:], ln_sh[:], start=True, stop=False)
                    pe.matmul(lnv_ps[:], mean_r[:], ln_sl[:], start=False, stop=True).then_inc(w1_pe, 1)
                if experts:
                    pe.matmul(mo_ps[:], eb_hi[:], gt[:], start=True, stop=False)
                    pe.matmul(mo_ps[:], eb_lo[:], gt[:], start=False, stop=False)
                for e in range(E):
                    if experts:
                        pe.wait_ge(xg_dve, q * E + (e + 1))
                        if e + 2 < E:
                            spread(q, e + 2)
                        pe.matmul(mo_ps[:], ew[:, e, :], xg[:, e % 3, :], start=False,
                                  stop=(e == E - 1)).then_inc(x_pe, 1)
                    if values and e == C2_AT:
                        if norm:
                            norm_center(v, t2_dve, (xf_dve, n + 2), c2_pe)
                        else:
                            norm_center(v, t2_dve, (xn2_dve, v), c2_pe)
                    if values and e == W2_AT:
                        norm_var(v, sq2, (ln1, n + 2 if norm else NBLK), w2_pe)

            def spread(q, e):
                pe.matmul(bc_ps[:, e % 2, :], sel_e[:, e, :], gt[:], start=True, stop=True).then_inc(g_pe, 1)

            def router(n, q, p, keys):
                pe.wait_ge(xn2_dve, q + 1)
                pe.wait_ge(d_dve, n if keys else NBLK)
                for i in range(TT):
                    mm = pe.matmul(row_ps[:, i * E:(i + 1) * E], xn2[:, p, i * C:(i + 1) * C], rw[:],
                                   start=True, stop=True)
                mm.then_inc(r_pe, 1)

            def turn_gates(q):
                pe.wait_ge(g16_dve, 2 * q + 2)
                at_least(pe, out_dve, q)
                for i in range(TT):
                    mm = pe.transpose(mo_ps[0:2 * E, i * C:(i + 1) * C], g16[:, i, :], ident[:])
                mm.then_inc(gt_pe, 1)

            walk(pe, it)

        @block.scalar
        def _(act):
            def norm_pre(n, c_pe, free, sq):
                act.wait_ge(c_pe, n + 1)
                at_least(act, *free)
                nc.scalar.activation(ln_sq[:], lnd_ps[:], ACT.Square).then_inc(sq, 1)

            def norm_post(n, w_pe, free, ln, rs):
                act.wait_ge(w_pe, n + 1)
                nc.scalar.activation(ln_l[:], lnv_ps[:], ACT.Ln, bias=epsc[:]).then_inc(ln, 1)
                act.wait_ge(ln, n + 1)
                at_least(act, *free)
                nc.scalar.activation(ln_r[:], ln_l[:], ACT.Exp, scale=-0.5).then_inc(rs, 1)

            def high(n, par):
                act.wait_ge(xf_dve, n + 1)
                at_least(act, v_pe, (n - 1) * HEADS)
                nc.scalar.copy(xn_hi[:, par, :], xf[:]).then_inc(hi_act, 1)

            nc.scalar.preload_act_table_set("natural_log_exp_and_others")
            act.wait_ge(cst3, 3)
            norm_pre(0, c1_pe, (w2_pe, 0), sq1)
            norm_post(0, w1_pe, (xn2_dve, 0), ln1, rs1)
            for g in range(2 * HEADS // TT):
                act.wait_ge(wt_pe, g + 1)
                dst = w_hi[:].rearrange("p h w c -> p (h w c)")[:, g * BANK:(g + 1) * BANK]
                nc.scalar.copy(dst, kv_ps[:, g % 2, :]).then_inc(wt_hi, 1)
            high(0, 0)

            def it(n, p, keys, values, experts, norm, new_rows, new_values):
                v, q = n - 1, n - 2

                nc.scalar.preload_act_table_set("silu_and_others")
                if keys:
                    at_least(act, s_pe, n)
                for h in range(HEADS):
                    if values:
                        act.wait_ge(v_pe, v * HEADS + (h + 1))
                        at_least(act, z_dve, v * HEADS + (h - 2))
                        nc.scalar.activation(sv[:, h % 3, :], kv_ps[:, 1 if keys else h % 2, :],
                                             ACT.Silu).then_inc(v_act, 1)
                    if experts and h == 5:
                        act.wait_ge(gate, q * GATE + 9)
                        nc.scalar.activation(th[:], dl[:], ACT.Tanh).then_inc(th_act, 1)
                    if keys:
                        act.wait_ge(k_pe, n * HEADS + (h + 1))
                        nc.scalar.activation(sk[:, h, :], kv_ps[:, 0 if values else h % 2, :],
                                             ACT.Silu).then_inc(k_act, 1)
                    if norm and h == 0:
                        loaded(act, n)
                        act.wait_ge(c1_pe, n + 1)
                        nc.scalar.copy(t_h[:], t[:, tok(n + 1)]).then_inc(tk_hi, 1)
                    if norm and h == 3:
                        norm_pre(n + 1, c1_pe, (w2_pe, n - 1), sq1)
                        act.wait_ge(sq1, n + 2)
                        nc.scalar.copy(ln_sh[:], ln_sq[:]).then_inc(sq_hi, 1)
                if experts:
                    turned(q)
                nc.scalar.preload_act_table_set("natural_log_exp_and_others")
                if norm:
                    norm_post(n + 1, w1_pe, (xn2_dve, n - 1), ln1, rs1)
                if keys:
                    act.wait_ge(d_dve, n + 1)
                    nc.scalar.activation(e_r[:], d_r[:], ACT.Exp).then_inc(e_act, 1)
                if norm:
                    high(n + 1, 1 - p)
                if keys:
                    act.wait_ge(u_dve, n + 1)
                    nc.scalar.activation(l_r[:], u_r[:], ACT.Ln).then_inc(lu_act, 1)
                if values:
                    norm_pre(v, c2_pe, (w1_pe, n + 2 if norm else NBLK), sq2)
                if keys:
                    act.wait_ge(l_dve, n + 1)
                    nc.scalar.activation(b_r[:], e_r[:], ACT.Exp).then_inc(b_act, 1)
                    act.wait_ge(b_act, n + 1)
                    at_least(act, rows_dve, 2 * n)
                    nc.scalar.activation(zr[:, 0, :], b_r[:], ACT.Identity, bias=zeros[:, 0:1],
                                         scale=low_rows[:]).then_inc(rows_act, 1)
                    nc.scalar.activation(a_r[:], b_r[:], ACT.Identity, bias=ones[:], scale=-1.0)
                    nc.scalar.activation(zr[:, 1, :], b_r[:], ACT.Identity, bias=low_rows[:],
                                         scale=neg_low[:]).then_inc(rows_act, 1)
                if values:
                    norm_post(v, w2_pe, (xf_dve, n + 2 if norm else NBLK), ln2, rs2)

            def turned(q):
                act.wait_ge(gt_pe, q + 1)
                nc.scalar.copy(gt[0:2 * E, :], mo_ps[0:2 * E, :]).then_inc(gt_act, 1)

            walk(act, it)

        @block.vector
        def _(dve):
            dve.wait_ge(cst3, 3)
            nc.vector.tensor_scalar(center_r[:], ident[:], -1.0 / C, None, ALU.add)
            nc.vector.tensor_scalar(mean_r[:], ident[:], 0.0, 1.0 / C, ALU.mult, ALU.add)
            nc.vector.tensor_scalar(center[:], ident[:], -1.0 / C, None, ALU.add).then_inc(cst3, 1)
            def norm_one(n, par):
                dve.wait_ge(rs1, n + 1)
                at_least(dve, hi_act, n)
                at_least(dve, lo_pool, n)
                nc.vector.tensor_tensor(xf[:], lnd_ps[:], ln_r[:], ALU.mult).then_inc(xf_dve, 1)

            norm_one(0, 0)
            for g in range(2 * HEADS // TT):
                dve.wait_ge(wt_hi, g + 1)
                sl_ = slice(g * BANK, (g + 1) * BANK)
                nc.vector.tensor_tensor(w_lo[:].rearrange("p h w c -> p (h w c)")[:, sl_], kv_ps[:, g % 2, :],
                                        w_hi[:].rearrange("p h w c -> p (h w c)")[:, sl_].bitcast(F32),
                                        ALU.subtract).then_inc(wt_lo, 1)
            dve.wait_ge(w_in, 16 * 6)
            for h in range(HEADS):
                r0 = QUAD * (h % 4) + h // 4
                nc.vector.tensor_tensor(sel_h[:, h, :], ident[:, r0:r0 + 1].to_broadcast([C, C]),
                                        ident[:, r0 + HALF:r0 + HALF + 1].to_broadcast([C, C]), ALU.add)
                for col in (h // 4, h // 4 + HALF):
                    nc.vector.tensor_copy(qz[:, h, col:col + 1], qcol[:, h:h + 1])
            for e in range(E):
                nc.vector.tensor_tensor(sel_e[:, e, :], ident[:, e:e + 1].to_broadcast([C, C]),
                                        ident[:, e + E:e + E + 1].to_broadcast([C, C]), ALU.add)
            nc.vector.tensor_reduce(low_rows[:], low_rows4[:], AX.X, ALU.add).then_inc(cst2, 1)
            nc.vector.tensor_reduce(neg_low[:], low_rows4[:], AX.X, ALU.add, negate=True).then_inc(cst2, 1)
            nc.vector.tensor_reduce(place_i[:], before[:], AX.X, ALU.add).then_inc(cst2, 1)
            nc.vector.tensor_copy(eb_hi[:], eb[:]).then_inc(cst2, 1)
            dve.wait_ge(cst2, 5)
            nc.vector.tensor_scalar(place_i[:], place_i[:], -5.0, None, ALU.add).then_inc(cst2, 1)
            nc.vector.tensor_tensor(eb_lo[:], eb[:], eb_hi[:].bitcast(F32), ALU.subtract).then_inc(cst3, 1)

            def gates(q, slot):
                def ready(k):
                    dve.wait_ge(gate, q * GATE + k)

                if slot == 0:
                    dve.wait_ge(r_pe, q + 1)
                    rb4 = rbias[:].unsqueeze(1).to_broadcast([C, TT, E])
                    nc.vector.tensor_tensor(lg[:], row_ps[:, 0:TT * E].rearrange("p (t e) -> p t e", t=TT), rb4,
                                            ALU.add).then_inc(gate, 1)
                    ready(1)
                    lj = lg[:].unsqueeze(2).to_broadcast([C, TT, E, E])
                    li = lg[:].unsqueeze(3).to_broadcast([C, TT, E, E])
                    nc.vector.tensor_tensor(ge[:], lj, li, ALU.is_ge).then_inc(gate, 1)
                if slot == 1:
                    ready(2)
                    nc.vector.tensor_tensor(gel[:], ge[:], before[:].unsqueeze(1).to_broadcast([C, TT, E, E]),
                                            ALU.mult).then_inc(gate, 1)
                if slot == 2:
                    ready(3)
                    nc.vector.tensor_reduce(r1[:], gel[:], AX.X, ALU.add).then_inc(gate, 1)
                    nc.vector.tensor_reduce(r2[:], gel[:].rearrange("p t i j -> p t j i"), AX.X,
                                            ALU.add).then_inc(gate, 1)
                if slot == 3:
                    ready(5)
                    nc.vector.tensor_tensor(rank[:], r1[:], r2[:], ALU.subtract).then_inc(gate, 1)
                if slot == 4:
                    ready(6)
                    nc.vector.tensor_tensor(pick[:], rank[:], place_i[:].unsqueeze(1).to_broadcast([C, TT, E]),
                                            ALU.is_lt).then_inc(gate, 1)
                if slot == 5:
                    ready(7)
                    nc.vector.tensor_tensor(sl[:], pick[:], lg[:], ALU.mult).then_inc(gate, 1)
                if slot == 6:
                    ready(8)
                    nc.vector.tensor_reduce(ssum[:], sl[:], AX.X, ALU.add).then_inc(g16_dve, 1)
                if slot == 7:
                    dve.wait_ge(g16_dve, 2 * q + 1)
                    nc.vector.scalar_tensor_tensor(out=dl[:], in0=ssum[:].unsqueeze(2).to_broadcast([C, TT, E]),
                                                   scalar=-0.5, in1=lg[:], op0=ALU.mult, op1=ALU.add).then_inc(gate, 1)
                if slot == 9:
                    dve.wait_ge(th_act, q + 1)
                    nc.vector.tensor_scalar(g1[:], th[:], 0.5, 0.5, ALU.mult, ALU.add).then_inc(gate, 1)
                if slot == 10:
                    ready(10)
                    nc.vector.tensor_tensor(g2[:], g1[:], pick[:], ALU.mult).then_inc(gate, 1)
                if slot == 11:
                    ready(11)
                    nc.vector.tensor_copy(ghr[:], g2[:]).then_inc(gate, 1)
                if slot == 12:
                    ready(12)
                    nc.vector.tensor_copy(g16[:, :, 0:E], ghr[:].bitcast(F32))
                    nc.vector.tensor_tensor(g16[:, :, E:2 * E], g2[:], ghr[:].bitcast(F32),
                                            ALU.subtract).then_inc(g16_dve, 1)

            def new_row(n):
                at_least(dve, bc_pe, n * HEADS)
                dve.wait_ge(rows_act, 2 * n + 1)
                nc.vector.tensor_tensor(new_w[:], b_r[:], zr[:, 0, :].bitcast(F32), ALU.subtract).then_inc(rows_dve, 1)

            def old_row(n):
                dve.wait_ge(rows_act, 2 * n + 2)
                nc.vector.tensor_tensor(old_w[:], a_r[:], zr[:, 1, :].bitcast(F32), ALU.subtract).then_inc(rows_dve, 1)

            def it(n, p, keys, values, experts, norm, new_rows, new_values):
                v, q = n - 1, n - 2
                for h in range(HEADS):
                    if values:
                        dve.wait_ge(v_act, v * HEADS + (h + 1))
                        dve.wait_ge(bcn_pe, v * HEADS + (h + 1))
                        at_least(dve, y_dve, v * HEADS + (h - 1))
                        nc.vector.tensor_tensor(z[:, h % 2, :], bc_ps[:, 0, :], sv[:, h % 3, :], ALU.mult).then_inc(z_dve, 1)
                    if experts:
                        gates(q, 2 * h)
                    if values:
                        dve.wait_ge(bc_pe, v * HEADS + (h + 1))
                        dve.wait_ge(z_dve, v * HEADS + (h + 1))
                        if h == 0:
                            at_least(dve, acc_pool, v * (HEADS - 1))
                        nc.vector.tensor_tensor_scan(y[:, h, :], bc_ps[:, 1, :], z[:, h % 2, :],
                                                     0.0 if new_values else y[:, h, TOK - 1:TOK],
                                                     ALU.mult, ALU.add).then_inc(y_dve, 1)
                    if experts:
                        gates(q, 2 * h + 1)

                def expert(e):
                    if experts:
                        dve.wait_ge(g_pe, q * E + (e + 1))
                        if e >= 3:
                            dve.wait_ge(x_pe, q * E + (e - 2))
                        nc.vector.tensor_tensor(xg[:, e % 3, :], bc_ps[:, e % 2, :], xn2[:, p, :], ALU.mult).then_inc(xg_dve, 1)

                expert(0)
                expert(1)
                if keys:
                    dve.wait_ge(s_pe, n + 1)
                    at_least(dve, m_dve, n)
                    nc.vector.tensor_tensor_scan(m_r[:], row_ps[:], zeros[:],
                                                 LOWEST if new_rows else m_r[:, TOK - 1:TOK],
                                                 ALU.max, ALU.add).then_inc(m_dve, 1)
                    dve.wait_ge(m_dve, n + 1)
                    at_least(dve, l_dve, n)
                    nc.vector.tensor_tensor(d_r[:], row_ps[:], m_r[:], ALU.subtract).then_inc(d_dve, 1)
                expert(2)
                expert(3)
                if norm:
                    norm_one(n + 1, 1 - p)
                if values:
                    dve.wait_ge(acc_pool, v * (HEADS - 1) + (HEADS - 1))
                    tv = t[:, tok(v)]
                    nc.vector.scalar_tensor_tensor(out=tv, in0=acc[:], scalar=1.0 / HEADS, in1=tv, op0=ALU.mult,
                                                   op1=ALU.add).then_inc(t2_dve, 1)
                if keys:
                    dve.wait_ge(e_act, n + 1)
                    at_least(dve, u_dve, n)
                    nc.vector.tensor_tensor_scan(u_r[:], e_r[:], zeros[:], 0.0 if new_rows else u_r[:, TOK - 1:TOK],
                                                 ALU.add, ALU.add).then_inc(u_dve, 1)
                expert(4)
                if keys:
                    dve.wait_ge(lu_act, n + 1)
                    nc.vector.tensor_tensor(e_r[:], d_r[:], l_r[:], ALU.subtract).then_inc(l_dve, 1)
                expert(5)
                expert(6)
                if keys:
                    new_row(n)
                expert(7)
                if keys:
                    old_row(n)
                if values:
                    dve.wait_ge(rs2, v + 1)
                    nc.vector.tensor_tensor(xn2[:, 1 - p, :], lnd_ps[:], ln_r[:], ALU.mult).then_inc(xn2_dve, 1)
                if experts:
                    dve.wait_ge(x_pe, q * E + E)
                    tq = t[:, tok(q)]
                    nc.vector.tensor_tensor(tq, mo_ps[:], tq, ALU.add).then_inc(out_dve, 1)

            walk(dve, it)


def hybrid_layers(nc, x, norm_w, norm_b, Wq, bq, Wk, bk, Wv, bv, Wo, bo, W_kv, q_proj, router_w, router_b,
                  expert_w, expert_b, out):
    B, _, H, W = x.shape
    t_dram = nc.dram_tensor("tokens", (C, B * H * W), F32, kind="Internal").ap()
    softmax_attention(nc, x, norm_w, norm_b, Wq, bq, Wk, bk, Wv, bv, Wo, bo, t_dram)
    scan_attention_and_experts(nc, t_dram, W_kv, q_proj, router_w, router_b, expert_w, expert_b, out)


_INS = ['x', 'L0_conv_norm_w', 'L0_conv_norm_b', 'L0_conv_Wq', 'L0_conv_bq', 'L0_conv_Wk', 'L0_conv_bk',
        'L0_conv_Wv', 'L0_conv_bv', 'L0_conv_Wo', 'L0_conv_bo', 'L1_attn_W_kv', 'L1_attn_q_proj',
        'L1_ffn_router_w', 'L1_ffn_router_b', 'L1_ffn_expert_w', 'L1_ffn_expert_b']
_OUTS = [((4, 128, 64, 64), 'float32')]


def kernel(**inputs):
    import numpy as _np
    import concourse.bacc as _bacc
    from concourse import mybir as _mybir
    from concourse.bass_utils import run_bass_kernel_spmd as _run

    nc = _bacc.Bacc("TRN2", target_bir_lowering=False, num_devices=1)
    arrays, args = {}, []
    for name in _INS:
        a = _np.ascontiguousarray(inputs[name])
        arrays[f"in_{name}_dram"] = a
        args.append(nc.dram_tensor(f"in_{name}_dram", a.shape, _mybir.dt.from_np(a.dtype), kind="ExternalInput").ap())
    for i, (shape, dtype) in enumerate(_OUTS):
        dt = _mybir.dt.from_np(_np.dtype(dtype))
        args.append(nc.dram_tensor(f"out_{i}_dram", shape, dt, kind="ExternalOutput").ap())
    hybrid_layers(nc, *args)
    r = _run(nc, [arrays], core_ids=[0])
    got = tuple(r.results[0][f"out_{i}_dram"] for i in range(len(_OUTS)))
    return got[0]
```
